# Optimizing a Trainium2 kernel written in Bass

```python
import numpy as np
import jax
import jax.numpy as jnp

def _softmax(x, axis=-1):
    return jax.nn.softmax(x, axis=axis)

def _gelu(x):
    return jax.nn.gelu(x, approximate=True)

def _silu(x):
    return jax.nn.silu(x)

def _sigmoid(x):
    return jax.nn.sigmoid(x)

def _layernorm(x, axis=-1, eps=1e-05):
    m = jnp.mean(x, axis=axis, keepdims=True)
    v = jnp.var(x, axis=axis, keepdims=True)
    return (x - m) / jnp.sqrt(v + eps)

def _scatter_add(tgt, idx, src, axis=0):
    return tgt.at[idx].add(src)

def _segment_sum(src, seg, n):
    return jax.ops.segment_sum(src, seg, n)
kernel_name = 'mk_conv_seq_d1_conv_nhwc128_r4_9134ee'

def setup_inputs(seed: int=0):
    np.random.seed(seed)
    _w = jnp.asarray

    def _rec_inputs():
        import jax
        import jax.numpy as jnp
        _gk = jax.random.key(seed)
        x = -0.000125 + 0.9999 * jax.random.normal(jax.random.fold_in(_gk, 1), (8, 16, 128, 32), jnp.float32)
        return x
    x = _rec_inputs()

    def _L0_conv_setup():
        import jax, jax.numpy as jnp
        import numpy as np
        DIM, HEADS = (32, 4)
        WH, WW = (4, 32)
        SH, SW = (2, 2)
        H, W, B = (16, 128, 8)
        N = WH * WW
        HD = DIM // HEADS
        SCALE = HD ** (-0.5)
        NHW, NWW = (H // WH, W // WW)
        NWIN = NHW * NWW

        def _rel_pos_index():
            coords = np.stack(np.meshgrid(np.arange(WH), np.arange(WW), indexing='ij'))
            flat = coords.reshape(2, -1)
            rel = (flat[:, :, None] - flat[:, None, :]).transpose(1, 2, 0)
            rel[:, :, 0] += WH - 1
            rel[:, :, 1] += WW - 1
            rel[:, :, 0] *= 2 * WW - 1
            return rel.sum(-1)

        def _attn_mask():
            img = np.zeros((H, W))
            cnt = 0
            for h in (slice(0, -WH), slice(-WH, -SH), slice(-SH, None)):
                for w in (slice(0, -WW), slice(-WW, -SW), slice(-SW, None)):
                    img[h, w] = cnt
                    cnt += 1
            mw = img.reshape(NHW, WH, NWW, WW).transpose(0, 2, 1, 3).reshape(-1, N)
            diff = mw[:, None, :] - mw[:, :, None]
            return np.where(diff != 0, -100.0, 0.0).astype(np.float32)
        _RPI = _rel_pos_index()
        _MASK = _attn_mask()

        def _layernorm(x, g, b):
            m = jnp.mean(x, axis=-1, keepdims=True)
            v = jnp.mean(jnp.square(x - m), axis=-1, keepdims=True)
            return (x - m) * jax.lax.rsqrt(v + 1e-05) * g + b
        key = jax.random.key(seed)
        ks = jax.random.split(key, 6)
        s = 0.02
        return {'x': jax.random.normal(ks[0], (B, H, W, DIM), jnp.float32), 'g1': jnp.ones((DIM,), jnp.float32), 'b1': jnp.zeros((DIM,), jnp.float32), 'qkv_w': jax.random.normal(ks[1], (DIM, 3 * DIM), jnp.float32) * s, 'qkv_b': jnp.zeros((3 * DIM,), jnp.float32), 'rpb': jax.random.normal(ks[2], ((2 * WH - 1) * (2 * WW - 1), HEADS), jnp.float32) * s, 'proj_w': jax.random.normal(ks[3], (DIM, DIM), jnp.float32) * s, 'proj_b': jnp.zeros((DIM,), jnp.float32), 'g2': jnp.ones((DIM,), jnp.float32), 'b2': jnp.zeros((DIM,), jnp.float32), 'fc1_w': jax.random.normal(ks[4], (DIM, 4 * DIM), jnp.float32) * s, 'fc1_b': jnp.zeros((4 * DIM,), jnp.float32), 'fc2_w': jax.random.normal(ks[5], (4 * DIM, DIM), jnp.float32) * s, 'fc2_b': jnp.zeros((DIM,), jnp.float32)}
    _L0_conv_all = _L0_conv_setup()
    _L0_conv_in = {k: v for k, v in _L0_conv_all.items() if k in ('g1', 'b1', 'qkv_w', 'qkv_b', 'rpb', 'proj_w', 'proj_b', 'g2', 'b2', 'fc1_w', 'fc1_b', 'fc2_w', 'fc2_b')}
    del _L0_conv_all
    return {'x': x, 'L0_conv_g1': _L0_conv_in['g1'], 'L0_conv_b1': _L0_conv_in['b1'], 'L0_conv_qkv_w': _L0_conv_in['qkv_w'], 'L0_conv_qkv_b': _L0_conv_in['qkv_b'], 'L0_conv_rpb': _L0_conv_in['rpb'], 'L0_conv_proj_w': _L0_conv_in['proj_w'], 'L0_conv_proj_b': _L0_conv_in['proj_b'], 'L0_conv_g2': _L0_conv_in['g2'], 'L0_conv_b2': _L0_conv_in['b2'], 'L0_conv_fc1_w': _L0_conv_in['fc1_w'], 'L0_conv_fc1_b': _L0_conv_in['fc1_b'], 'L0_conv_fc2_w': _L0_conv_in['fc2_w'], 'L0_conv_fc2_b': _L0_conv_in['fc2_b']}

def reference(x, L0_conv_g1, L0_conv_b1, L0_conv_qkv_w, L0_conv_qkv_b, L0_conv_rpb, L0_conv_proj_w, L0_conv_proj_b, L0_conv_g2, L0_conv_b2, L0_conv_fc1_w, L0_conv_fc1_b, L0_conv_fc2_w, L0_conv_fc2_b):
    import jax
    import jax.numpy as jnp

    def _L0_conv_ref(x, g1, b1, qkv_w, qkv_b, rpb, proj_w, proj_b, g2, b2, fc1_w, fc1_b, fc2_w, fc2_b):
        import jax, jax.numpy as jnp
        import numpy as np
        DIM, HEADS = (32, 4)
        WH, WW = (4, 32)
        SH, SW = (2, 2)
        H, W, B = (16, 128, 8)
        N = WH * WW
        HD = DIM // HEADS
        SCALE = HD ** (-0.5)
        NHW, NWW = (H // WH, W // WW)
        NWIN = NHW * NWW

        def _rel_pos_index():
            coords = np.stack(np.meshgrid(np.arange(WH), np.arange(WW), indexing='ij'))
            flat = coords.reshape(2, -1)
            rel = (flat[:, :, None] - flat[:, None, :]).transpose(1, 2, 0)
            rel[:, :, 0] += WH - 1
            rel[:, :, 1] += WW - 1
            rel[:, :, 0] *= 2 * WW - 1
            return rel.sum(-1)

        def _attn_mask():
            img = np.zeros((H, W))
            cnt = 0
            for h in (slice(0, -WH), slice(-WH, -SH), slice(-SH, None)):
                for w in (slice(0, -WW), slice(-WW, -SW), slice(-SW, None)):
                    img[h, w] = cnt
                    cnt += 1
            mw = img.reshape(NHW, WH, NWW, WW).transpose(0, 2, 1, 3).reshape(-1, N)
            diff = mw[:, None, :] - mw[:, :, None]
            return np.where(diff != 0, -100.0, 0.0).astype(np.float32)
        _RPI = _rel_pos_index()
        _MASK = _attn_mask()

        def _layernorm(x, g, b):
            m = jnp.mean(x, axis=-1, keepdims=True)
            v = jnp.mean(jnp.square(x - m), axis=-1, keepdims=True)
            return (x - m) * jax.lax.rsqrt(v + 1e-05) * g + b
        mask = jnp.asarray(_MASK)
        y = _layernorm(x, g1, b1)
        y = jnp.roll(y, (-SH, -SW), axis=(1, 2))
        xw = y.reshape(B, NHW, WH, NWW, WW, DIM).transpose(0, 1, 3, 2, 4, 5)
        xw = xw.reshape(B * NWIN, N, DIM)
        qkv = (xw @ qkv_w + qkv_b).reshape(B * NWIN, N, 3, HEADS, HD)
        qkv = qkv.transpose(2, 0, 3, 1, 4)
        q, k, v = (qkv[0] * SCALE, qkv[1], qkv[2])
        attn = jnp.einsum('bhid,bhjd->bhij', q, k)
        bias = rpb[_RPI.reshape(-1)].reshape(N, N, HEADS).transpose(2, 0, 1)
        attn = attn + bias[None]
        attn = attn.reshape(B, NWIN, HEADS, N, N) + mask[None, :, None]
        attn = jax.nn.softmax(attn.reshape(B * NWIN, HEADS, N, N), axis=-1)
        o = jnp.einsum('bhij,bhjd->bhid', attn, v)
        o = o.transpose(0, 2, 1, 3).reshape(B * NWIN, N, DIM)
        o = o @ proj_w + proj_b
        o = o.reshape(B, NHW, NWW, WH, WW, DIM).transpose(0, 1, 3, 2, 4, 5)
        o = o.reshape(B, H, W, DIM)
        o = jnp.roll(o, (SH, SW), axis=(1, 2))
        x = x + o
        z = _layernorm(x, g2, b2)
        z = jax.nn.gelu(z @ fc1_w + fc1_b, approximate=False) @ fc2_w + fc2_b
        return x + z

    def _gn(v, G=32, eps=1e-05):
        B_, H_, W_, C_ = v.shape
        g = v.reshape(B_, H_, W_, G, C_ // G)
        m = jnp.mean(g, axis=(1, 2, 4), keepdims=True)
        s = jnp.var(g, axis=(1, 2, 4), keepdims=True)
        return ((g - m) / jnp.sqrt(s + eps)).reshape(v.shape)

    def _ln_c(v, eps=1e-06):
        m = jnp.mean(v, axis=-1, keepdims=True)
        s = jnp.var(v, axis=-1, keepdims=True)
        return (v - m) / jnp.sqrt(s + eps)

    def _ln_t(v, eps=1e-05):
        m = jnp.mean(v, axis=-1, keepdims=True)
        s = jnp.var(v, axis=-1, keepdims=True)
        return (v - m) / jnp.sqrt(s + eps)

    def _to_tokens(v):
        B_, H_, W_, C_ = v.shape
        return v.reshape(B_, H_ * W_, C_)

    def _from_tokens(t, like):
        return t.reshape(like.shape)
    x = _L0_conv_ref(x, L0_conv_g1, L0_conv_b1, L0_conv_qkv_w, L0_conv_qkv_b, L0_conv_rpb, L0_conv_proj_w, L0_conv_proj_b, L0_conv_g2, L0_conv_b2, L0_conv_fc1_w, L0_conv_fc1_b, L0_conv_fc2_w, L0_conv_fc2_b)
    return x

_drawn_inputs = setup_inputs


def setup_inputs(seed=0):
    import zlib

    import numpy as np

    out = dict(_drawn_inputs(seed))
    spreads = {'L0_conv_g1': (1.0, 0.6),
     'L0_conv_b1': (0.0, 0.8),
     'L0_conv_qkv_b': (0.0, 0.738),
     'L0_conv_proj_b': (0.0, 0.1),
     'L0_conv_g2': (1.0, 0.6),
     'L0_conv_b2': (0.0, 0.8),
     'L0_conv_fc1_b': (0.0, 0.592),
     'L0_conv_fc2_b': (0.0, 0.1)}
    factors = {'L0_conv_qkv_w': 8.0,
     'L0_conv_rpb': 8.0,
     'L0_conv_proj_w': 6.383,
     'L0_conv_fc1_w': 4.332,
     'L0_conv_fc2_w': 3.306}
    for name, (base, spread) in spreads.items():
        noise = np.random.default_rng([zlib.crc32(name.encode()), seed]).standard_normal(out[name].shape)
        drawn = base * np.exp(spread * noise) if base else spread * noise
        out[name] = jnp.asarray(drawn.astype(out[name].dtype))
    for name, factor in factors.items():
        out[name] = (out[name] * factor).astype(out[name].dtype)
    return out
```

```python
from contextlib import ExitStack

import concourse.bass as bass
from concourse import mybir

B, H, W, C = 8, 16, 128, 32
HEADS, HD = 4, 8
WH, WW, SHIFT = 4, 32, 2
TOK = WH * WW
GW = W // WW
NG = H // WH
WPI = GW * NG
NWIN = B * WPI
NGRP = B * NG
F = 4 * C
HTOK = HEADS * TOK
IMG = WPI * C
SCALE = HD ** -0.5
EPS = 1e-5
NPART = 3
SLOT_PARTS = ((0, 0, 0, 1, 1, 2), (0, 1, 2, 0, 1, 0))
NSLOT = len(SLOT_PARTS[0])
KROWS = HD * NSLOT
MROWS = 2
HALF = WPI // 2 * TOK

_WIDTHS = dict(g1=1, b1=1, g2=1, b2=1, qkb=1, qks=1, fc1b=1, fc2b=1, colscale=128, wqk=256, wv=128,
               ident=128, flip=128, vb=128, wp=128, sel=HEADS * HD + HEADS, pb=C, mask=3 * 128, w1=GW * F, w2=C)
PCOL, _at = {}, 0
for _n, _w in _WIDTHS.items():
    PCOL[_n] = (_at, _at + _w)
    _at += _w
NPCOL = _at

LEAD = 8
HEAD_STEPS = 5
LOOPS = 3
BODY = 2 * WPI
TAIL_STEPS = 5


def swin_kernel(nc, x, params, rel1, rel2, scratch, out):
    fp32, bf16 = mybir.dt.float32, mybir.dt.bfloat16
    ALU, ACT, AX = mybir.AluOpType, mybir.ActivationFunctionType, mybir.AxisListType

    with ExitStack() as ctx:
        def sb(name, shape, dt=fp32):
            return ctx.enter_context(nc.sbuf_tensor(name, shape, dt))

        def sem(name):
            return ctx.enter_context(nc.semaphore(name))

        X = sb("X", [128, NWIN * C])
        par = sb("par", [128, NPCOL])

        def P(name):
            a, b = PCOL[name]
            return par[:, a:b]

        rel_i = sb("rel_i", [128, 4, HTOK])
        rel_j = sb("rel_j", [128, 4, HTOK])
        wqk_c = sb("wqk_c", [128, 256])
        wqk = sb("wqk_s", [128, 256])
        wv = sb("wv_s", [128, 128])
        w1 = sb("w1_s", [128, GW * F])
        b1wide = sb("b1wide", [128, 128])
        qk_bias = sb("qk_bias", [128, 1])
        v_bias = sb("v_bias", [128, 128])
        f_bias = sb("f_bias", [128, 1])
        neghalf, per_channel, eps = sb("neghalf", [128, WPI]), sb("per_channel", [128, WPI]), sb("eps", [128, WPI])
        q_rows = sb("q_rows", [128, 2, HEADS * WPI * TOK], bf16)
        k_rows = sb("k_rows", [128, 2, HEADS * WPI * TOK], bf16)
        parts = sb("parts", [128, 2, NPART, 2 * 512], bf16)
        rest = sb("rest", [128, 2, 512])
        ssum = sb("ssum", [128, WPI])
        mean = sb("mean", [128, WPI])
        vsum = sb("vsum", [128, WPI])
        var = sb("var", [128, WPI])
        rstd = sb("rstd", [128, WPI])
        xc = sb("xc", [128, IMG])
        sq = sb("sq", [128, IMG])
        yn = sb("yn", [128, IMG])
        yT = sb("yT", [128, 2, 512])
        va = sb("va", [128, 2, WPI * HEADS * 32])
        s1sb = sb("s1sb", [128, 4, HTOK])
        negm = sb("negm", [128, 2, HEADS * GW])
        m_hi = sb("m_hi", [HEADS * GW, 2, 128], bf16)
        m_mid = sb("m_mid", [HEADS * GW, 2, 128], bf16)
        prob = sb("prob", [128, 4, HTOK])
        oT = sb("oT", [128, 2, 512])
        rec = sb("rec", [128, GW * HEADS])
        onorm = sb("onorm", [128, 128])
        onT = sb("onT", [128, 128])
        hT = sb("hT", [128, 8, 512])
        zT = sb("zT", [128, 2, 512])
        mT2 = sb("mT2", [128, 512])
        res = sb("res", [128, 2, IMG])

        def bank(name):
            return ctx.enter_context(nc.psum_tensor(name, [128, 512], fp32))

        ps1 = [bank("ps1a"), bank("ps1b")]
        ps2 = [bank("ps2a"), bank("ps2b")]
        pav = bank("pav")
        pch = bank("pch")
        pst = [bank("pst0"), bank("pst1")]

        d_x0, d_xr, d_par, d_rel = sem("d_x0"), sem("d_xr"), sem("d_par"), sem("d_rel")
        d_scr, d_mrow, d_out = sem("d_scr"), sem("d_mrow"), [sem("d_out0"), sem("d_out1")]
        d_qk = [sem("d_qk0"), sem("d_qk1")]
        w_ready, b_ps, b_ready, rel_ready, zero_ready = (sem("w_ready"), sem("b_ps"), sem("b_ready"),
                                                         sem("rel_ready"), sem("zero_ready"))
        credits_ready, rel_ps = sem("credits_ready"), sem("rel_ps")
        sum_done, mean_done, xc_done, sq_done, var_done = (sem("sum_done"), sem("mean_done"), sem("xc_done"),
                                                           sem("sq_done"), sem("var_done"))
        veps_done, rstd_done, yn_done, xpb_done = sem("veps_done"), sem("rstd_done"), sem("yn_done"), sem("xpb_done")
        yTp_done, yT_done, qk_done, hi_done, rest_done = (sem("yTp_done"), sem("yT_done"), sem("qk_done"),
                                                          sem("hi_done"), sem("rest_done"))
        mid_done, lo_done, vp_done, va_done = sem("mid_done"), sem("lo_done"), sem("vp_done"), sem("va_done")
        s1_done, s1_copied, s1_biased, max_done = sem("s1_done"), sem("s1_copied"), sem("s1_biased"), sem("max_done")
        mT_done, mhi_done, mmid_done = sem("mT_done"), sem("mhi_done"), sem("mmid_done")
        s2_done, s2_biased, exp_done, av_done = sem("s2_done"), sem("s2_biased"), sem("exp_done"), sem("av_done")
        oT_done, otok_done, rec_done, on_done = sem("oT_done"), sem("otok_done"), sem("rec_done"), sem("on_done")
        onTp_done, onT_done, proj_done, x2_done = (sem("onTp_done"), sem("onT_done"), sem("proj_done"),
                                                   sem("x2_done"))
        z_done, zTp_done, zT_done, fc1_done, gelu_done = (sem("z_done"), sem("zTp_done"), sem("zT_done"),
                                                          sem("fc1_done"), sem("gelu_done"))
        fc2_done, mT2_done, mlp_done, res_done = sem("fc2_done"), sem("mT2_done"), sem("mlp_done"), sem("res_done")
        sum2_done, mean2_done, xc2_done, sq2_done, var2_done = (sem("sum2_done"), sem("mean2_done"),
                                                                sem("xc2_done"), sem("sq2_done"), sem("var2_done"))
        veps2_done, rstd2_done = sem("veps2_done"), sem("rstd2_done")

        CREDIT = {s1_copied: 2, max_done: 4, s2_biased: 2, av_done: 4, s2_done: 2 * WPI, mT_done: 2,
                  d_scr: 2 * 192, d_mrow: 2 * 32, d_qk[0]: 2 * 32, d_qk[1]: 2 * 32, lo_done: 2,
                  rest_done: 2, va_done: 2, oT_done: 1, otok_done: 2, x2_done: 1, mmid_done: 0,
                  yn_done: 0, yTp_done: 2, vp_done: 2,
                  zTp_done: 1, zT_done: 1, gelu_done: 4, fc2_done: 2, mT2_done: 1, res_done: 1, mlp_done: 1,
                  d_out[0]: 16, d_out[1]: 16}

        def after(eng, s, count):
            if isinstance(count, int) and count <= 0:
                return
            eng.wait_ge(s, count + CREDIT.get(s, 0))

        def after_all(eng, *waits):
            values = [c + CREDIT.get(s, 0) for s, c in waits]
            values = [v if isinstance(v, int) else eng.to_reg(v) for v in values]
            for (s, c), v in zip(waits, values):
                if not isinstance(c, int) or c > 0:
                    eng.wait_ge(s, v)

        block = ctx.enter_context(nc.Block())

        def live(it, index, n):
            return not isinstance(it, int) or 0 <= index < n

        def drive(eng, step):
            for j in range(HEAD_STEPS):
                step(0, j)
            with eng.Fori(0, LOOPS) as it:
                for j in range(HEAD_STEPS, HEAD_STEPS + BODY):
                    step(it, j)
            for j in range(HEAD_STEPS + LOOPS * BODY, NWIN + TAIL_STEPS):
                step(0, j)

        def img_cols(it, b):
            return bass.ds(it * (2 * IMG) + b * IMG, IMG)

        def win_col(jw):
            g, wx = (jw // GW) % NG, jw % GW
            return wx * NG * TOK + g * TOK

        def kind(jw):
            return 2 * ((jw // GW) % NG == NG - 1) + (jw % GW == GW - 1)

        @block.sync
        def _(sp):
            sp.dma_start(X[:, 0:IMG], x[:, 0:IMG]).then_inc(d_x0, 16)
            sp.dma_start(par[:, 0:PCOL["wp"][0]], params[:, 0:PCOL["wp"][0]]).then_inc(d_par, 16)
            sp.dma_start(par[:, PCOL["wp"][0]:], params[:, PCOL["wp"][0]:]).then_inc(d_par, 16)
            sp.dma_start(X[:, IMG:], x[:, IMG:]).then_inc(d_xr, 16)
            for t, src in enumerate((rel1, rel2)):
                for y in range(WH):
                    runs = bass.AP(src.tensor, (y * HEADS * WH) * (2 * WW - 1),
                                   [[1, WW], [2 * WW - 1, HEADS * WH], [1, WW]])
                    sp.dma_start(s1sb[WW * y:WW * (y + 1), t, :].rearrange("p (a c) -> p a c", c=WW),
                                 runs).then_inc(d_rel, 16)
            sp.wait_ge(credits_ready, 1)

            def scatter_parts(it, b):
                after_all(sp, (lo_done, it * 4 + 2 * (b + 1)),
                          (d_qk[0], it * 64 + 32 * (b - 1)), (d_qk[1], it * 64 + 32 * (b - 1)))
                for qk in range(2):
                    for w in range(2):
                        rows = slice(64 * w + 32 * qk, 64 * w + 32 * qk + 32)
                        for a, z in ((0, 3), (3, 5), (5, 6)):
                            if qk:
                                src = parts[rows, b % 2, 0:z - a, :]
                            else:
                                one = SLOT_PARTS[0][a]
                                src = parts[rows, b % 2, one:one + 1, :].to_broadcast([32, z - a, 2 * 512])
                            sp.dma_start(scratch[b % 2, qk, :, a:z, w, :], src).then_inc(d_scr, 16)

            def gather_rows(it, b):
                after_all(sp, (d_scr, it * 384 + 192 * (b + 1)),
                          (s2_done, it * 32 + 16 * (b - 1)))
                for w in range(2):
                    for qk, rows in enumerate((q_rows, k_rows)):
                        dst = rows[0:KROWS, b % 2, :].rearrange("p (h w n) -> p h w n", h=HEADS, w=2)[:, :, w, :]
                        src = scratch[b % 2, qk].rearrange("(h d) s w n -> (d s) h w n", h=HEADS)[:, :, w, :]
                        sp.dma_start(dst, src).then_inc(d_qk[w], 16)

            scatter_parts(0, 0)
            gather_rows(0, 0)
            scatter_parts(0, 1)
            with sp.Fori(0, LOOPS) as it:
                for b in range(2):
                    gather_rows(it, b + 1)
                    scatter_parts(it, b + 2)
            gather_rows(0, 7)

            def store(it, b):
                after(sp, res_done, it * 2 + b + 1)
                sp.dma_start(out[:, bass.ds(it * (2 * IMG) + b * IMG, IMG)], res[:, b % 2, :]).then_inc(d_out[b], 16)

            with sp.Fori(0, B // 2) as it:
                for b in range(2):
                    store(it, b)
            for b in range(2):
                after(sp, d_out[b], 16 * (B // 2))

        @block.gpsimd
        def _(pool):
            for s, n in CREDIT.items():
                if n:
                    pool.sem_inc(s, n)
            pool.sem_inc(credits_ready, 5)
            for t, v in ((neghalf, -0.5), (per_channel, 1.0 / C), (eps, EPS)):
                pool.memset(t[:], v).then_inc(zero_ready, 1)
            pool.wait_ge(zero_ready, 3)
            pool.memset(k_rows[32:64, 0, :], 1.0).then_inc(zero_ready, 1)
            pool.memset(k_rows[32:64, 1, :], 1.0).then_inc(zero_ready, 1)

            def center(it, b, cnt, s_sum, s_mean, s_xc, s_sq, s_free, free_count):
                xs = X[:, img_cols(it, b)].rearrange("p (w c) -> p w c", c=C)
                v = lambda t: t[:].rearrange("p (w c) -> p w c", c=C)
                pool.wait_ge(s_sum, cnt)
                if s_free is not None:
                    after(pool, s_free, free_count)
                pool.tensor_tensor(mean[:], ssum[:], per_channel[:], ALU.mult).then_inc(s_mean, 1)
                pool.wait_ge(s_mean, cnt)
                pool.tensor_tensor(v(xc), xs, mean[:].unsqueeze(2).to_broadcast([128, WPI, C]),
                                   ALU.subtract).then_inc(s_xc, 1)
                pool.wait_ge(s_xc, cnt)
                pool.tensor_tensor(sq[:], xc[:], xc[:], ALU.mult).then_inc(s_sq, 1)

            def normalise(it, b, cnt, s_var, s_veps, s_rstd, s_y):
                v = lambda t: t[:].rearrange("p (w c) -> p w c", c=C)
                pool.wait_ge(s_var, cnt)
                pool.tensor_tensor(var[:], vsum[:], per_channel[:], ALU.mult).then_inc(s_veps, 1)
                pool.wait_ge(s_veps, 2 * cnt - 1)
                pool.tensor_tensor(var[:], var[:], eps[:], ALU.add).then_inc(s_veps, 1)
                pool.wait_ge(s_veps, 2 * cnt)
                pool.tensor_tensor(rstd[:], var[:], neghalf[:], ALU.pow).then_inc(s_rstd, 1)
                pool.wait_ge(s_rstd, cnt)
                pool.tensor_tensor(v(yn), v(xc), rstd[:].unsqueeze(2).to_broadcast([128, WPI, C]),
                                   ALU.mult).then_inc(s_y, 1)

            def ln1_center(it, b):
                center(it, b, it * 2 + b + 1, sum_done, mean_done, xc_done, sq_done, None, None)

            def ln1_scale(it, b):
                after(pool, yTp_done, it * 2 + b)
                normalise(it, b, it * 2 + b + 1, var_done, veps_done, rstd_done, yn_done)

            def low_part(it, b, p):
                after(pool, mid_done, it * 4 + 2 * b + p + 1)
                pool.tensor_tensor(parts[:, b % 2, 2, 512 * p:512 * (p + 1)], rest[:, p, :],
                                   parts[:, b % 2, 1, 512 * p:512 * (p + 1)], ALU.subtract).then_inc(lo_done, 1)

            def add_proj_bias(it, b):
                xs = X[:, img_cols(it, b)].rearrange("p (w c) -> p w c", c=C)
                pool.tensor_tensor(xs, xs, P("pb").unsqueeze(1).to_broadcast([128, WPI, C]),
                                   ALU.add).then_inc(xpb_done, 1)

            def bias_scores(it, j):
                pool.wait_ge(s1_copied, it * 32 + j + 1 + CREDIT[s1_copied])
                pool.tensor_tensor(s1sb[:, j % 4, :], s1sb[:, j % 4, :], rel_i[:, kind(j), :],
                                   ALU.add).then_inc(s1_biased, 1)

            pool.wait_ge(d_par, 32)
            pool.wait_ge(zero_ready, 5)
            for b in range(2):
                ln1_center(0, b)
                ln1_scale(0, b)
                for p in range(2):
                    low_part(0, b, p)
                if b == 0:
                    add_proj_bias(0, 0)
            pool.wait_ge(rel_ready, 8)
            for j in range(LEAD):
                bias_scores(0, j)

            def step(it, j):
                b, w = j // WPI, j % WPI
                if live(it, j + LEAD, NWIN):
                    bias_scores(it, j + LEAD)
                if w == 3 and live(it, b + 1, B):
                    add_proj_bias(it, b + 1)
                if w == 6 and live(it, b + 2, B):
                    ln1_center(it, b + 2)
                if w == 8 and live(it, b + 2, B):
                    ln1_scale(it, b + 2)
                if w in (12, 13) and live(it, b + 2, B):
                    low_part(it, b + 2, w - 12)

            drive(pool, step)

            with pool.Fori(0, B // 2) as it:
                for b in range(2):
                    cnt = it * 2 + b + 1
                    center(it, b, cnt, sum2_done, mean2_done, xc2_done, sq2_done, None, None)
                    after(pool, zTp_done, it * 2 + b)
                    normalise(it, b, cnt, var2_done, veps2_done, rstd2_done, z_done)

        @block.vector
        def _(dve):
            dve.memset(va[:], 0.0).then_inc(w_ready, 1)
            dve.wait_ge(w_ready, 1)
            dve.memset(va[:].rearrange("p a (n c) -> p (a n) c", c=32)[:, :, HD:HD + 1], 1.0).then_inc(w_ready, 1)
            dve.wait_ge(d_par, 32)
            dve.tensor_tensor(wqk_c[:].rearrange("p (a n) -> p a n", a=2), P("wqk").rearrange("p (a n) -> p a n", a=2),
                              P("colscale").unsqueeze(1).to_broadcast([128, 2, 128]), ALU.mult).then_inc(w_ready, 1)
            dve.tensor_copy(b1wide[:], P("b1").to_broadcast([128, 128])).then_inc(w_ready, 1)
            dve.tensor_scalar(wv[:], P("wv"), P("g1"), None, ALU.mult).then_inc(w_ready, 1)
            dve.wait_ge(w_ready, 5)
            dve.tensor_scalar(wqk[:], wqk_c[:], P("g1"), None, ALU.mult).then_inc(w_ready, 1)
            dve.wait_ge(d_x0, 16)

            def sums(it, b, s):
                dve.tensor_reduce(ssum[:], X[:, img_cols(it, b)].rearrange("p (w c) -> p w c", c=C),
                                  AX.X, ALU.add).then_inc(s, 1)

            def square_sums(cnt, s_in, s_out):
                dve.wait_ge(s_in, cnt)
                dve.tensor_reduce(vsum[:], sq[:].rearrange("p (w c) -> p w c", c=C), AX.X, ALU.add).then_inc(s_out, 1)

            sums(0, 0, sum_done)
            dve.tensor_scalar(w1[:], P("w1"), P("g2"), None, ALU.mult).then_inc(w_ready, 1)
            dve.wait_ge(b_ps, 1)
            dve.scalar_tensor_tensor(qk_bias[:], P("qkb"), P("qks"), pst[0][:, 0:1], ALU.mult,
                                     ALU.add).then_inc(b_ready, 1)
            dve.tensor_tensor(v_bias[:], pst[0][:, 128:256], P("vb"), ALU.add).then_inc(b_ready, 1)
            dve.tensor_tensor(f_bias[:], pst[0][:, 256:257], P("fc1b"), ALU.add).then_inc(b_ready, 1)

            def remainder(it, b, p):
                after(dve, lo_done, it * 4 + 2 * (b - 1) + p + 1)
                dve.wait_ge(hi_done, it * 4 + 2 * b + p + 1)
                dve.scalar_tensor_tensor(rest[:, p, :], pst[1 - p][:], qk_bias[:],
                                         parts[:, b % 2, 0, 512 * p:512 * (p + 1)], ALU.add,
                                         ALU.subtract).then_inc(rest_done, 1)

            def values(it, b):
                dve.wait_ge(vp_done, it * 2 + b + 1 + CREDIT[vp_done])
                after(dve, av_done, it * 32 + 16 * (b - 1))
                dve.tensor_tensor(
                    va[:, b % 2, :].rearrange("p (g n c) -> p g n c", g=NG, c=32)[:, :, :, 0:HD],
                    pst[1][:].rearrange("p (g n c) -> p g n c", g=NG, c=HD),
                    v_bias[:].rearrange("p (n c) -> p n c", c=HD).unsqueeze(1).to_broadcast([128, NG, GW * HEADS, HD]),
                    ALU.add).then_inc(va_done, 1)

            def row_max(it, j):
                if j % GW == 0:
                    after(dve, mT_done, it * 8 + j // GW - 1)
                dve.wait_ge(s1_biased, it * 32 + j + 1)
                dve.tensor_reduce(negm[:, (j // GW) % 2, :].rearrange("p (h w) -> p h w", h=HEADS)[:, :, j % GW],
                                  s1sb[:, j % 4, :].rearrange("p (h n) -> p h n", h=HEADS), AX.X, ALU.max,
                                  negate=True).then_inc(max_done, 1)

            def max_parts(it, k):
                after(dve, mT_done, it * 8 + k + 1)
                after(dve, d_mrow, it * 256 + 32 * (k - 1))
                t = pch[0:HEADS * GW, 0:128]
                dve.tensor_copy(m_hi[:, k % 2, :], t).then_inc(mhi_done, 1)
                dve.wait_ge(mhi_done, it * 8 + k + 1)
                dve.tensor_tensor(m_mid[:, k % 2, :], t, m_hi[:, k % 2, :], ALU.subtract).then_inc(mmid_done, 1)

            for b in range(2):
                if b:
                    dve.wait_ge(d_xr, 16)
                    dve.wait_ge(xc_done, 1)
                    sums(0, 1, sum_done)
                square_sums(b + 1, sq_done, var_done)
                for p in range(2):
                    remainder(0, b, p)
            for t, dst in enumerate((rel_i, rel_j)):
                dve.wait_ge(rel_ps, t + 1)
                dve.tensor_copy(dst[:, 0, :], ps2[t][:]).then_inc(rel_ready, 1)
                for m in range(3):
                    a = PCOL["mask"][0] + 128 * m
                    dve.tensor_tensor(dst[:, m + 1, :].rearrange("p (h n) -> p h n", h=HEADS),
                                      ps2[t][:].rearrange("p (h n) -> p h n", h=HEADS),
                                      par[:, a:a + 128].unsqueeze(1).to_broadcast([128, HEADS, 128]),
                                      ALU.add).then_inc(rel_ready, 1)
            values(0, 0)
            for j in range(LEAD - 1):
                row_max(0, j)
                if j == 4:
                    max_parts(0, 0)

            def step(it, j):
                b, w, k, i = j // WPI, j % WPI, j // GW, j % GW
                if live(it, j, NWIN):
                    dve.wait_ge(s2_done, it * 32 + j + 1 + CREDIT[s2_done])
                    after(dve, av_done, it * 32 + j - 3)
                    dve.tensor_tensor(prob[:, j % 4, :], ps2[j % 2][:], rel_j[:, kind(j), :],
                                      ALU.add).then_inc(s2_biased, 1)
                if live(it, j + LEAD - 1, NWIN):
                    row_max(it, j + LEAD - 1)
                if w == 4 and live(it, b + 1, B):
                    values(it, b + 1)
                if w == 5 and live(it, b + 2, B):
                    sums(it, b + 2, sum_done)
                if w == 7 and live(it, b + 2, B):
                    square_sums(it * 2 + b + 3, sq_done, var_done)
                if w in (11, 12) and live(it, b + 2, B):
                    remainder(it, b + 2, w - 11)
                if i == 0 and live(it, k - 2, NGRP):
                    dve.wait_ge(proj_done, it * 8 + k - 1)
                    dve.wait_ge(xpb_done, it * 2 + (k - 2) // NG + 1)
                    xs = X[:, bass.ds(it * (2 * IMG) + (k - 2) * GW * C, GW * C)]
                    dve.tensor_tensor(xs, xs, pch[:, 0:128], ALU.add).then_inc(x2_done, 1)
                if i == 1 and live(it, k + 1, NGRP):
                    max_parts(it, k + 1)
                if i == 2 and live(it, k - 1, NGRP):
                    after(dve, otok_done, it * 8 + k)
                    o = pch[:, 0:256].rearrange("p (w n) -> p w n", w=GW)
                    dve.reciprocal(rec[:].rearrange("p (w h) -> p w h", w=GW),
                                   o[:, :, HEADS * HD:HEADS * HD + HEADS]).then_inc(rec_done, 1)
                    dve.wait_ge(rec_done, it * 8 + k)
                    dve.tensor_tensor(onorm[:].rearrange("p (w h d) -> p w h d", w=GW, h=HEADS),
                                      o[:, :, 0:HEADS * HD].rearrange("p w (h d) -> p w h d", h=HEADS),
                                      rec[:].rearrange("p (w h) -> p w h", w=GW).unsqueeze(3)
                                      .to_broadcast([128, GW, HEADS, HD]), ALU.mult).then_inc(on_done, 1)

            drive(dve, step)

            dve.wait_ge(yn_done, B)

            def ln2_sums(it, b):
                cnt = it * 2 + b
                after(dve, x2_done, it * 8 + NG * (b + 1))
                dve.wait_ge(var2_done, cnt) if not isinstance(cnt, int) or cnt else None
                sums(it, b, sum2_done)
                square_sums(cnt + 1, sq2_done, var2_done)

            def mlp_out(it, b):
                after(dve, fc2_done, it * 2 + b + 1)
                after(dve, mlp_done, it * 2 + b)
                dve.tensor_scalar(mT2[:], pav[:], P("fc2b"), None, ALU.add).then_inc(mT2_done, 1)

            def add_residual(it, b):
                dve.wait_ge(mlp_done, it * 2 + b + 1 + CREDIT[mlp_done])
                after(dve, d_out[b % 2], it * 16 + 16 * (b // 2))
                dve.tensor_tensor(res[:, b % 2, :], pch[:], X[:, img_cols(it, b)], ALU.add).then_inc(res_done, 1)

            ln2_sums(0, 0)
            ln2_sums(0, 1)
            mlp_out(0, 0)
            with dve.Fori(0, LOOPS) as it:
                for b in range(2):
                    ln2_sums(it, b + 2)
                    add_residual(it, b)
                    mlp_out(it, b + 1)
            add_residual(0, 6)
            mlp_out(0, 7)
            add_residual(0, 7)

        @block.scalar
        def _(act):
            act.wait_ge(credits_ready, 2)

            def copy_yT(it, b):
                act.wait_ge(yTp_done, it * 2 + b + 1 + CREDIT[yTp_done])
                after(act, vp_done, it * 2 + b - 1)
                act.activation(yT[:, b % 2, :], pst[0][:], ACT.Copy).then_inc(yT_done, 1)

            def high_part(it, b, p):
                act.wait_ge(qk_done, it * 4 + 2 * b + p + 1)
                after(act, d_scr, it * 384 + 192 * (b - 1))
                act.activation(parts[:, b % 2, 0, 512 * p:512 * (p + 1)], pst[1 - p][:], ACT.Identity,
                               bias=qk_bias[:]).then_inc(hi_done, 1)

            def middle_part(it, b, p):
                act.wait_ge(rest_done, it * 4 + 2 * b + p + 1 + CREDIT[rest_done])
                act.activation(parts[:, b % 2, 1, 512 * p:512 * (p + 1)], rest[:, p, :],
                               ACT.Copy).then_inc(mid_done, 1)

            def copy_s1(it, j):
                act.wait_ge(s1_done, it * 32 + j + 1)
                after(act, max_done, it * 32 + j - 3)
                act.activation(s1sb[:, j % 4, :], ps1[j % 2][:], ACT.Copy).then_inc(s1_copied, 1)

            def send_max(it, k):
                act.wait_ge(mmid_done, it * 8 + k + 1)
                g = k % NG
                for r, t in enumerate((m_hi, m_mid)):
                    dst = q_rows[KROWS + r:KROWS + r + 1, (k // NG) % 2, :] \
                        .rearrange("p (a g n) -> p a g n", g=NG, n=TOK)[:, :, g, :]
                    act.dma_start(dst, t[:, k % 2, :]).then_inc(d_mrow, 16)

            act.wait_ge(b_ready, 3)
            act.wait_ge(rel_ps, 2)
            for b in range(2):
                copy_yT(0, b)
                for p in range(2):
                    high_part(0, b, p)
                for p in range(2):
                    middle_part(0, b, p)
            for j in range(LEAD):
                copy_s1(0, j)
                if j == 6:
                    send_max(0, 0)

            def step(it, j):
                b, w, k, i = j // WPI, j % WPI, j // GW, j % GW
                if live(it, j + LEAD, NWIN):
                    copy_s1(it, j + LEAD)
                if i == 1 and live(it, k - 1, NGRP):
                    act.wait_ge(av_done, it * 32 + GW * k + CREDIT[av_done])
                    after(act, otok_done, it * 8 + k - 2)
                    act.activation(oT[:, (k - 1) % 2, :], pav[:], ACT.Copy).then_inc(oT_done, 1)
                if i == 2 and live(it, k + 1, NGRP):
                    send_max(it, k + 1)
                if live(it, j, NWIN):
                    act.wait_ge(s2_biased, it * 32 + j + 1 + CREDIT[s2_biased])
                    act.activation(prob[:, j % 4, :], prob[:, j % 4, :], ACT.Exp).then_inc(exp_done, 1)
                if i == 3 and live(it, k - 1, NGRP):
                    act.wait_ge(onTp_done, it * 8 + k)
                    act.activation(onT[:], pch[:, 0:128], ACT.Copy).then_inc(onT_done, 1)
                if w == 10 and live(it, b + 2, B):
                    copy_yT(it, b + 2)
                if w in (11, 12) and live(it, b + 2, B):
                    high_part(it, b + 2, w - 11)
                if w in (12, 13) and live(it, b + 2, B):
                    middle_part(it, b + 2, w - 12)

            drive(act, step)

            def copy_zT(it, b):
                act.wait_ge(zTp_done, it * 2 + b + 1 + CREDIT[zTp_done])
                act.activation(zT[:, b % 2, :], pst[0][:], ACT.Copy).then_inc(zT_done, 1)

            def gelu(it, b, w):
                act.wait_ge(fc1_done, it * 8 + 4 * b + w + 1)
                after(act, fc2_done, it * 2 + b - 1)
                act.activation(hT[:, 4 * (b % 2) + w, :], (ps1 + ps2)[w][:], ACT.Gelu,
                               bias=f_bias[:]).then_inc(gelu_done, 1)

            copy_zT(0, 0)
            with act.Fori(0, LOOPS) as it:
                for b in range(2):
                    gelu(it, b, 0)
                    gelu(it, b, 1)
                    copy_zT(it, b + 1)
                    gelu(it, b, 2)
                    gelu(it, b, 3)
            for b in (6, 7):
                for w in range(GW):
                    gelu(0, b, w)
                    if w == 1 and b == 6:
                        copy_zT(0, 7)

        @block.tensor
        def _(pe):
            pe.wait_ge(credits_ready, 3)
            pe.wait_ge(w_ready, 5)
            pe.matmul(pst[0][:, 0:1], wqk_c[:, 0:128], P("b1"), start=True, stop=True)
            pe.matmul(pst[0][:, 128:256], b1wide[:], P("wv"), start=True, stop=True)
            pe.matmul(pst[0][:, 256:257], P("w1")[:, 0:128], P("b2"), start=True, stop=True).then_inc(b_ps, 1)

            def transpose_y(it, b):
                after(pe, rest_done, it * 4 + 2 * b)
                pe.wait_ge(yn_done, it * 2 + b + 1)
                for g in range(NG):
                    mm = pe.transpose(pst[0][:, 128 * g:128 * (g + 1)], yn[:, 128 * g:128 * (g + 1)], P("ident"))
                mm.then_inc(yTp_done, 1)

            def project_qk(it, b, p, values):
                if p == 0:
                    after(pe, va_done, values)
                    after(pe, rest_done, it * 4 + 2 * b - 1)
                pe.wait_ge(yT_done, it * 2 + b + 1)
                pe.matmul(pst[1 - p][:], wqk[:, 128 * p:128 * (p + 1)], yT[:, b % 2, :], start=True,
                          stop=True).then_inc(qk_done, 1)

            def project_v(it, b, halves):
                after(pe, rest_done, halves)
                for g in range(NG):
                    mm = pe.matmul(pst[1][:, 128 * g:128 * (g + 1)], yT[:, b % 2, 128 * g:128 * (g + 1)], wv[:],
                                   start=True, stop=True)
                mm.then_inc(vp_done, 1)

            def s1(it, j):
                if (j // GW) % NG == 0 and j % 2 == 0:
                    w = (j % GW) // 2
                    after(pe, d_qk[w], it * 64 + 32 * (j // WPI + 1))
                after(pe, s1_copied, it * 32 + j - 1)
                c = win_col(j)
                for h in range(HEADS):
                    a = HALF * 2 * h + c
                    mm = pe.matmul(ps1[j % 2][:, 128 * h:128 * (h + 1)],
                                   q_rows[0:KROWS, (j // WPI) % 2, a:a + TOK],
                                   k_rows[0:KROWS, (j // WPI) % 2, a:a + TOK], start=True, stop=True)
                mm.then_inc(s1_done, 1)

            def s2(it, j):
                if j % GW == 0:
                    after(pe, d_mrow, it * 256 + 32 * (j // GW + 1))
                after(pe, s2_biased, it * 32 + j - 1)
                c = win_col(j)
                for h in range(HEADS):
                    a = HALF * 2 * h + c
                    mm = pe.matmul(ps2[j % 2][:, 128 * h:128 * (h + 1)],
                                   k_rows[0:KROWS + MROWS, (j // WPI) % 2, a:a + TOK],
                                   q_rows[0:KROWS + MROWS, (j // WPI) % 2, a:a + TOK], start=True, stop=True)
                mm.then_inc(s2_done, 1)

            def av(it, j):
                k, i = j // GW, j % GW
                if i == 0:
                    after(pe, oT_done, it * 8 + k)
                    if (k % NG) == 0:
                        after(pe, va_done, it * 2 + k // NG + 1)
                pe.wait_ge(exp_done, it * 32 + j + 1)
                for h in range(HEADS):
                    a = ((j % WPI) * HEADS + h) * 32
                    mm = pe.matmul(pav[32 * h:32 * (h + 1), 128 * i:128 * (i + 1)],
                                   va[:, (j // WPI) % 2, a:a + 32], prob[:, j % 4, 128 * h:128 * (h + 1)],
                                   start=True, stop=True)
                mm.then_inc(av_done, 1)

            def transpose_max(it, k):
                after(pe, x2_done, it * 8 + k - 2)
                pe.wait_ge(max_done, it * 32 + GW * (k + 1) + CREDIT[max_done])
                pe.transpose(pch[0:HEADS * GW, 0:128], negm[:, k % 2, :], P("ident")).then_inc(mT_done, 1)

            pe.wait_ge(w_ready, 6)
            pe.wait_ge(b_ready, 3)
            pe.wait_ge(d_par, 32)
            pe.wait_ge(d_rel, 8 * 16)
            for t in range(2):
                pe.matmul(ps2[t][:], P("flip"), s1sb[:, t, :], start=True, stop=True).then_inc(rel_ps, 1)
            for b in range(2):
                transpose_y(0, b)
                for p in range(2):
                    project_qk(0, b, p, 0)
            project_v(0, 0, 4)
            for j in range(LEAD):
                s1(0, j)
                if j == 5:
                    transpose_max(0, 0)

            def step(it, j):
                b, w, k, i = j // WPI, j % WPI, j // GW, j % GW
                if live(it, j + LEAD, NWIN):
                    s1(it, j + LEAD)
                if live(it, j, NWIN):
                    s2(it, j)
                if i == 0 and live(it, k - 2, NGRP):
                    pe.wait_ge(onT_done, it * 8 + k - 1)
                    pe.matmul(pch[:, 0:128], onT[:], P("wp"), start=True, stop=True).then_inc(proj_done, 1)
                if i == 1 and live(it, k + 1, NGRP):
                    transpose_max(it, k + 1)
                if i == 2 and live(it, k - 1, NGRP):
                    pe.wait_ge(oT_done, it * 8 + k + CREDIT[oT_done])
                    pe.wait_ge(mmid_done, it * 8 + k + 2 if not isinstance(it, int) else min(k + 2, NGRP))
                    after(pe, x2_done, it * 8 + k - 1)
                    for u in range(GW):
                        mm = pe.matmul(pch[:, 64 * u:64 * u + HEADS * HD + HEADS],
                                       oT[:, (k - 1) % 2, 128 * u:128 * (u + 1)], P("sel"), start=True, stop=True)
                    mm.then_inc(otok_done, 1)
                if i == 3 and live(it, k - 1, NGRP):
                    pe.wait_ge(on_done, it * 8 + k)
                    pe.transpose(pch[:, 0:128], onorm[:], P("ident")).then_inc(onTp_done, 1)
                if w == 4 and live(it, b + 1, B):
                    project_v(it, b + 1, it * 4 + 2 * b + 4)
                if w == 9 and live(it, b + 2, B):
                    transpose_y(it, b + 2)
                if w in (10, 11) and live(it, b + 2, B):
                    project_qk(it, b + 2, w - 10, it * 2 + b + 2)
                if live(it, j - 1, NWIN):
                    av(it, j - 1)

            drive(pe, step)

            after(pe, x2_done, NGRP)

            def transpose_z(it, b):
                after(pe, zT_done, it * 2 + b)
                pe.wait_ge(z_done, it * 2 + b + 1)
                for g in range(NG):
                    mm = pe.transpose(pst[0][:, 128 * g:128 * (g + 1)], yn[:, 128 * g:128 * (g + 1)], P("ident"))
                mm.then_inc(zTp_done, 1)

            def fc1(it, b, w):
                if w == 0:
                    pe.wait_ge(zT_done, it * 2 + b + 1 + CREDIT[zT_done])
                after(pe, gelu_done, it * 8 + 4 * (b - 1) + w + 1)
                pe.matmul((ps1 + ps2)[w][:], w1[:, F * w:F * (w + 1)], zT[:, b % 2, :], start=True,
                          stop=True).then_inc(fc1_done, 1)

            def fc2(it, b):
                after(pe, gelu_done, it * 8 + 4 * (b + 1))
                after(pe, mT2_done, it * 2 + b)
                for w in range(GW):
                    mm = pe.matmul(pav[32 * w:32 * (w + 1), :], P("w2"), hT[:, 4 * (b % 2) + w, :], start=True,
                                   stop=True)
                mm.then_inc(fc2_done, 1)

            def transpose_out(it, b):
                after(pe, mT2_done, it * 2 + b + 1)
                after(pe, res_done, it * 2 + b)
                for g in range(NG):
                    mm = pe.transpose(pch[:, 128 * g:128 * (g + 1)], mT2[:, 128 * g:128 * (g + 1)], P("ident"))
                mm.then_inc(mlp_done, 1)

            def image(it, b, first=False, last=False):
                fc1(it, b, 0)
                fc1(it, b, 1)
                if not first:
                    fc2(it, b - 1)
                if not last:
                    transpose_z(it, b + 1)
                fc1(it, b, 2)
                if not first:
                    transpose_out(it, b - 1)
                fc1(it, b, 3)

            transpose_z(0, 0)
            image(0, 0, first=True)
            with pe.Fori(0, LOOPS) as it:
                for b in (1, 2):
                    image(it, b)
            image(0, 7, last=True)
            fc2(0, 7)
            transpose_out(0, 7)


def _to_tokens(x):
    import numpy as np
    x = np.roll(x, (-SHIFT, -SHIFT), axis=(1, 2))
    x = x.reshape(B, NG, WH, GW, WW, C).transpose(2, 4, 0, 1, 3, 5)
    return np.ascontiguousarray(x.reshape(TOK, NWIN * C))


def _from_tokens(y):
    import numpy as np
    y = y.reshape(WH, WW, B, NG, GW, C).transpose(2, 3, 0, 4, 1, 5).reshape(B, H, W, C)
    return np.ascontiguousarray(np.roll(y, (SHIFT, SHIFT), axis=(1, 2)))


def _masks():
    import numpy as np
    y, x = np.divmod(np.arange(TOK), WW)
    below, right = (y >= WH - SHIFT).astype(int), (x >= WW - SHIFT).astype(int)
    return [np.where(r[:, None] != r[None, :], -100.0, 0.0).astype(np.float32)
            for r in (right, below, 2 * below + right)]


def _pack(p):
    import numpy as np
    a = np.zeros((128, NPCOL), np.float32)

    def put(name, v):
        lo, hi = PCOL[name]
        a[:, lo:hi] = v

    for n, k in (("g1", "g1"), ("b1", "b1"), ("g2", "g2"), ("b2", "b2"), ("fc2b", "fc2_b")):
        put(n, np.tile(p[k], GW)[:, None])
    put("fc1b", p["fc1_b"][:, None])
    put("qkb", np.tile(p["qkv_b"][0:2 * C], 2)[:, None])
    scale = np.tile(np.repeat([SCALE, 1.0], C), 2).astype(np.float32)
    put("qks", scale[:, None])
    put("colscale", scale[None, :])
    put("vb", np.tile(p["qkv_b"][2 * C:], GW)[None, :])
    put("pb", p["proj_b"][None, :])
    put("ident", np.eye(128, dtype=np.float32))
    put("flip", np.kron(np.eye(WH, dtype=np.float32), np.eye(WW, dtype=np.float32)[::-1]))
    put("mask", np.concatenate(_masks(), 1))
    put("w2", p["fc2_w"])
    wqk, wv, wp = (a[:, PCOL[n][0]:PCOL[n][1]] for n in ("wqk", "wv", "wp"))
    w1, sel = (a[:, PCOL[n][0]:PCOL[n][1]] for n in ("w1", "sel"))
    for w in range(GW):
        rows = slice(C * w, C * (w + 1))
        half, half_w = w % 2, w // 2
        wqk[rows, 128 * half + 64 * half_w:128 * half + 64 * half_w + 64] = p["qkv_w"][:, 0:2 * C]
        wv[rows, C * w:C * (w + 1)] = p["qkv_w"][:, 2 * C:]
        wp[rows, C * w:C * (w + 1)] = p["proj_w"]
        w1[rows, F * w:F * (w + 1)] = p["fc1_w"]
    for h in range(HEADS):
        for d in range(HD):
            sel[32 * h + d, HD * h + d] = 1.0
        sel[32 * h + HD, HEADS * HD + h] = 1.0
    return a


def _runs(rpb):
    import numpy as np
    t = rpb.T.reshape(HEADS, 2 * WH - 1, 2 * WW - 1)
    return [np.ascontiguousarray(np.stack([s[:, WH - 1 - y:2 * WH - 1 - y, :] for y in range(WH)]))
            for s in (t[:, ::-1, ::-1], t)]


def kernel(**inputs):
    import numpy as np
    import concourse.bacc as bacc
    from concourse.bass_utils import run_bass_kernel_spmd

    p = {k.removeprefix("L0_conv_"): np.asarray(v) for k, v in inputs.items()}
    rel_i, rel_j = _runs(p["rpb"])
    arrays = {"x_tok": _to_tokens(p["x"]), "params": _pack(p), "rel_i_runs": rel_i, "rel_j_runs": rel_j}
    nc = bacc.Bacc("TRN2", target_bir_lowering=False, num_devices=1)
    ins = [nc.dram_tensor(k, v.shape, mybir.dt.float32, kind="ExternalInput").ap() for k, v in arrays.items()]
    scratch = nc.dram_tensor("slots", (2, 2, C, NSLOT, 2, HALF), mybir.dt.bfloat16, kind="Internal").ap()
    out = nc.dram_tensor("y_tok", (TOK, NWIN * C), mybir.dt.float32, kind="ExternalOutput").ap()
    swin_kernel(nc, *ins, scratch, out)
    r = run_bass_kernel_spmd(nc, [arrays], core_ids=[0])
    return _from_tokens(r.results[0]["y_tok"])
```

```python
from contextlib import ExitStack

import concourse.bass as bass
from concourse import mybir

B, H, W, C = 8, 16, 128, 32
HEADS, HD = 4, 8
WH, WW, SHIFT = 4, 32, 2
TOK = WH * WW
GW = W // WW
NG = H // WH
WPI = GW * NG
NWIN = B * WPI
NGRP = B * NG
F = 4 * C
HTOK = HEADS * TOK
IMG = WPI * C
SCALE = HD ** -0.5
EPS = 1e-5
NPART = 3
SLOT_PARTS = ((0, 0, 0, 1, 2, 1), (2, 1, 0, 0, 0, 1))
NSLOT = len(SLOT_PARTS[0])
KROWS = HD * NSLOT
MROWS = 2
HALF = WPI // 2 * TOK

_WIDTHS = dict(g1=1, b1=1, g2=1, b2=1, qkb=1, qks=1, fc1b=1, fc2b=1, colscale=128, wqk=256, wv=128,
               ident=128, flip=128, vb=128, wp=128, sel=HEADS * HD + HEADS, pb=C, mask=3 * 128, w1=GW * F, w2=C)
PCOL, _at = {}, 0
for _n, _w in _WIDTHS.items():
    PCOL[_n] = (_at, _at + _w)
    _at += _w
NPCOL = _at

ONES_BF16 = 1 + 0x3F80 / 2 ** 23
LEAD = 8
EXP_LAG, AV_LAG = 3, 4
HEAD_STEPS = 8
POOL_WINDOWS = (1, 3, 5, 7, 9, 13, 15)
NPROB = 8
LOOPS = 3
BODY = 2 * WPI
TAIL_STEPS = 8


def swin_kernel(nc, x, params, rel1, rel2, scratch, out):
    fp32, bf16 = mybir.dt.float32, mybir.dt.bfloat16
    ALU, ACT, AX = mybir.AluOpType, mybir.ActivationFunctionType, mybir.AxisListType

    with ExitStack() as ctx:
        def sb(name, shape, dt=fp32):
            return ctx.enter_context(nc.sbuf_tensor(name, shape, dt))

        def sem(name):
            return ctx.enter_context(nc.semaphore(name))

        X = sb("X", [128, NWIN * C])
        par = sb("par", [128, NPCOL])

        def P(name):
            a, b = PCOL[name]
            return par[:, a:b]

        rel_i = sb("rel_i", [128, 4, HTOK], bf16)
        rel_j = sb("rel_j", [128, 4, HTOK])
        ident_b = sb("ident_b", [128, 128], bf16)
        wqk_c = sb("wqk_c", [128, 256])
        wqk = sb("wqk_s", [128, 256])
        wv = sb("wv_s", [128, 128])
        w1 = sb("w1_s", [128, GW * F])
        b1wide = sb("b1wide", [128, 128])
        qk_bias = sb("qk_bias", [128, 1])
        v_bias = sb("v_bias", [128, 128])
        f_bias = sb("f_bias", [128, 1])
        neghalf = sb("neghalf", [128, WPI])
        q_rows = sb("q_rows", [128, 2, HEADS * WPI * TOK], bf16)
        k_rows = sb("k_rows", [128, 2, HEADS * WPI * TOK], bf16)
        parts = sb("parts", [128, 2, NPART, 2 * 512], bf16)
        rest = sb("rest", [128, 2, 512])
        ssum = sb("ssum", [128, 2, WPI])
        mean = sb("mean", [128, 2, WPI])
        vsum = sb("vsum", [128, 2, WPI])
        var = sb("var", [128, 2, WPI])
        rstd = sb("rstd", [128, 2, WPI])
        xc = sb("xc", [128, 2, IMG])
        sq = sb("sq", [128, 2, IMG])
        yn = sb("yn", [128, 2, IMG])
        yT = sb("yT", [128, 2, 512])
        va = sb("va", [128, 2, WPI * HEADS * 32])
        negm = sb("negm", [128, 2, HEADS * GW])
        m_hi = sb("m_hi", [HEADS * GW, 2, 128], bf16)
        m_mid = sb("m_mid", [HEADS * GW, 2, 128], bf16)
        prob = sb("prob", [128, NPROB, HTOK])
        oT = sb("oT", [128, 2, 512])
        rec = sb("rec", [128, GW * HEADS])
        onorm = sb("onorm", [128, 128])
        onT = sb("onT", [128, 128])
        hT = k_rows[:, 0, :].bitcast(fp32).rearrange("p (w n) -> p w n", n=512)
        mT2 = sb("mT2", [128, 512])
        res = sb("res", [128, 2, IMG])

        def bank(name):
            return ctx.enter_context(nc.psum_tensor(name, [128, 512], fp32))

        ps1 = [bank("ps1a"), bank("ps1b")]
        ps2 = [bank("ps2a"), bank("ps2b")]
        pav = bank("pav")
        pch = bank("pch")
        pst = [bank("pst0"), bank("pst1")]

        d_x0, d_x1, d_xr, d_par, d_rel = sem("d_x0"), sem("d_x1"), sem("d_xr"), sem("d_par"), sem("d_rel")
        d_scr, d_out = sem("d_scr"), [sem("d_out0"), sem("d_out1")]
        d_mrow = [sem("d_mrow0"), sem("d_mrow1")]
        d_qk = [sem("d_qk0"), sem("d_qk1")]
        w_ready, b_ps, b_ready, rel_ready, zero_ready = (sem("w_ready"), sem("b_ps"), sem("b_ready"),
                                                         sem("rel_ready"), sem("zero_ready"))
        credits_ready, rel_ps, ident_ready = sem("credits_ready"), sem("rel_ps"), sem("ident_ready")
        sum_done, mean_done, xc_done, sq_done, var_done = (sem("sum_done"), sem("mean_done"), sem("xc_done"),
                                                           sem("sq_done"), sem("var_done"))
        veps_done, rstd_done, yn_done, xpb_done = sem("veps_done"), sem("rstd_done"), sem("yn_done"), sem("xpb_done")
        yTp_done, yT_done, qk_done, hi_done, rest_done = (sem("yTp_done"), sem("yT_done"), sem("qk_done"),
                                                          sem("hi_done"), sem("rest_done"))
        mid_done, lo_done, vp_done, va_done = sem("mid_done"), sem("lo_done"), sem("vp_done"), sem("va_done")
        s1_done, max_done = sem("s1_done"), sem("max_done")
        mT_done, mhi_done, mmid_done = sem("mT_done"), sem("mhi_done"), sem("mmid_done")
        s2_done, dve_biased = sem("s2_done"), sem("dve_biased")
        s2_copied, pool_biased = sem("s2_copied"), sem("pool_biased")
        exp_done, av_done = sem("exp_done"), sem("av_done")
        oT_done, otok_done, rec_done, on_done = sem("oT_done"), sem("otok_done"), sem("rec_done"), sem("on_done")
        onTp_done, onT_done, proj_done, x2_done = (sem("onTp_done"), sem("onT_done"), sem("proj_done"),
                                                   sem("x2_done"))
        fc1_done, gelu_done = sem("fc1_done"), sem("gelu_done")
        fc2_done, mT2_done, mlp_done, res_done = sem("fc2_done"), sem("mT2_done"), sem("mlp_done"), sem("res_done")

        CREDIT = {max_done: 2, av_done: 4, s2_done: 2 * WPI, mT_done: 2,
                  d_scr: 2 * 96, d_mrow[0]: 32, d_mrow[1]: 32, d_qk[0]: 2 * 32, d_qk[1]: 2 * 32, lo_done: 2,
                  rest_done: 2, va_done: 2, oT_done: 1, otok_done: 2, x2_done: 1, yTp_done: 2, vp_done: 2,
                  gelu_done: 4, fc2_done: 2, mT2_done: 1, res_done: 1, mlp_done: 1,
                  d_out[0]: 16, d_out[1]: 16}

        def after(eng, s, count):
            if isinstance(count, int) and count <= 0:
                return
            eng.wait_ge(s, count + CREDIT.get(s, 0))

        def after_all(eng, *waits):
            values = [c + CREDIT.get(s, 0) for s, c in waits]
            values = [v if isinstance(v, int) else eng.to_reg(v) for v in values]
            for (s, c), v in zip(waits, values):
                if not isinstance(c, int) or c > 0:
                    eng.wait_ge(s, v)

        block = ctx.enter_context(nc.Block())

        def live(it, index, n):
            return not isinstance(it, int) or 0 <= index < n

        def staged(it, j, at, n):
            b = (j - at) // WPI + 2
            return [b] if (j - at) % WPI == 0 and b >= 2 and live(it, b, n) else []

        def drive(eng, step):
            for j in range(HEAD_STEPS):
                step(0, j)
            with eng.Fori(0, LOOPS) as it:
                for j in range(HEAD_STEPS, HEAD_STEPS + BODY):
                    step(it, j)
            for j in range(HEAD_STEPS + LOOPS * BODY, NWIN + TAIL_STEPS):
                step(0, j)

        def drive_images(eng, image):
            with eng.Fori(0, 2) as it:
                image(it, 1)
                image(it, 2)
            for b in range(5, B + 1):
                image(0, b)

        def norm_cols(it, n):
            return img_cols(it, n % B)

        def img_cols(it, b):
            return bass.ds(it * (2 * IMG) + b * IMG, IMG)

        def win_col(jw):
            g, wx = (jw // GW) % NG, jw % GW
            return wx * NG * TOK + g * TOK

        def max_bank(k):
            return pst[(1, 1, 0, 0)[k % NG]]

        def by_pool(jw):
            return jw % WPI in POOL_WINDOWS and jw < NWIN - LEAD

        def path_count(it, jw):
            if isinstance(it, int):
                return sum(by_pool(v) == by_pool(jw) for v in range(jw + 1))
            same = [w for w in range(WPI) if (w in POOL_WINDOWS) == by_pool(jw)]
            return it * (2 * len(same)) + jw // WPI * len(same) + sum(w <= jw % WPI for w in same)

        def kind(jw):
            return 2 * ((jw // GW) % NG == NG - 1) + (jw % GW == GW - 1)

        @block.sync
        def _(sp):
            sp.dma_start(X[:, 0:IMG], x[:, 0:IMG]).then_inc(d_x0, 16)
            sp.dma_start(X[:, IMG:2 * IMG], x[:, IMG:2 * IMG]).then_inc(d_x1, 16)
            sp.dma_start(par[:, 0:PCOL["wp"][0]], params[:, 0:PCOL["wp"][0]]).then_inc(d_par, 16)
            sp.dma_start(par[:, PCOL["wp"][0]:], params[:, PCOL["wp"][0]:]).then_inc(d_par, 16)
            for t, src in enumerate((rel1, rel2)):
                for y in range(WH):
                    runs = bass.AP(src.tensor, (y * HEADS * WH) * (2 * WW - 1),
                                   [[1, WW], [2 * WW - 1, HEADS * WH], [1, WW]])
                    sp.dma_start(prob[WW * y:WW * (y + 1), t, :].rearrange("p (a c) -> p a c", c=WW),
                                 runs).then_inc(d_rel, 16)
            sp.dma_start(X[:, 2 * IMG:], x[:, 2 * IMG:]).then_inc(d_xr, 16)
            sp.wait_ge(credits_ready, 1)

            def scatter_parts(it, b):
                after_all(sp, (d_qk[0], it * 64 + 32 * (b - 1)), (d_qk[1], it * 64 + 32 * (b - 1)))
                for part, done in enumerate((hi_done, mid_done, lo_done)):
                    after(sp, done, it * 4 + 2 * (b + 1))
                    for qk in range(2):
                        rows = slice(64 * qk, 64 * qk + 64)
                        slots = [i for i, own in enumerate(SLOT_PARTS[qk]) if own == part]
                        every = slots[1] - slots[0] if len(slots) > 1 else 1
                        src = parts[rows, b % 2, part:part + 1, :].to_broadcast([64, len(slots), 2 * 512])
                        dst = scratch[b % 2, qk, :, :, slots[0]:slots[-1] + 1:every, :] \
                            .rearrange("w r s n -> (w r) s n")
                        sp.dma_start(dst, src).then_inc(d_scr, 16)

            def gather_rows(it, b):
                after_all(sp, (d_scr, it * 192 + 96 * (b + 1)),
                          (s2_done, it * 32 + 16 * (b - 1)))
                for w in range(2):
                    for qk, rows in enumerate((q_rows, k_rows)):
                        dst = rows[0:KROWS, b % 2, :].rearrange("p (h w n) -> p h w n", h=HEADS, w=2)[:, :, w, :]
                        src = scratch[b % 2, qk, w].rearrange("(h d) s n -> (d s) h n", h=HEADS)
                        sp.dma_start(dst, src).then_inc(d_qk[w], 16)

            scatter_parts(0, 0)
            sp.wait_ge(zero_ready, 3)
            gather_rows(0, 0)
            scatter_parts(0, 1)
            sp.wait_ge(zero_ready, 5)
            with sp.Fori(0, LOOPS) as it:
                for b in range(2):
                    gather_rows(it, b + 1)
                    scatter_parts(it, b + 2)
            gather_rows(0, 7)

            def store(it, b):
                after(sp, res_done, it * 2 + b + 1)
                sp.dma_start(out[:, bass.ds(it * (2 * IMG) + b * IMG, IMG)], res[:, b % 2, :]).then_inc(d_out[b], 16)

            with sp.Fori(0, B // 2) as it:
                for b in range(2):
                    store(it, b)
            for b in range(2):
                after(sp, d_out[b], 16 * (B // 2))

        @block.gpsimd
        def _(pool):
            for s, n in CREDIT.items():
                if n:
                    pool.sem_inc(s, n)
            pool.sem_inc(credits_ready, 5)
            pool.memset(neghalf[:], -0.5).then_inc(zero_ready, 1)
            pool.wait_ge(zero_ready, 1)

            def fill_rows(b):
                pool.memset(k_rows[:, b, :].bitcast(fp32), ONES_BF16).then_inc(zero_ready, 1)
                pool.memset(q_rows[:, b, :].bitcast(fp32), 0.0).then_inc(zero_ready, 1)

            fill_rows(0)

            def center(it, n):
                xs = X[:, norm_cols(it, n)].rearrange("p (w c) -> p w c", c=C)
                pool.wait_ge(mean_done, it * 2 + n + 1)
                if n >= 2:
                    pool.wait_ge(yn_done, it * 2 + n - 1)
                pool.tensor_tensor(xc[:, n % 2, :].rearrange("p (w c) -> p w c", c=C), xs,
                                   mean[:, n % 2, :].unsqueeze(2).to_broadcast([128, WPI, C]),
                                   ALU.subtract).then_inc(xc_done, 1)

            def scale(it, n):
                v = lambda t: t[:, n % 2, :].rearrange("p (w c) -> p w c", c=C)
                pool.wait_ge(veps_done, it * 2 + n + 1)
                pool.tensor_tensor(rstd[:, n % 2, :], var[:, n % 2, :], neghalf[:], ALU.pow).then_inc(rstd_done, 1)
                pool.wait_ge(rstd_done, it * 2 + n + 1)
                after(pool, yTp_done, it * 2 + n - 1)
                pool.tensor_tensor(v(yn), v(xc), rstd[:, n % 2, :].unsqueeze(2).to_broadcast([128, WPI, C]),
                                   ALU.mult).then_inc(yn_done, 1)

            def low_part(it, b, p):
                after(pool, mid_done, it * 4 + 2 * b + p + 1)
                pool.tensor_tensor(parts[:, b % 2, 2, 512 * p:512 * (p + 1)], rest[:, p, :],
                                   parts[:, b % 2, 1, 512 * p:512 * (p + 1)], ALU.subtract).then_inc(lo_done, 1)

            def add_proj_bias(it, b):
                xs = X[:, img_cols(it, b)].rearrange("p (w c) -> p w c", c=C)
                pool.tensor_tensor(xs, xs, P("pb").unsqueeze(1).to_broadcast([128, WPI, C]),
                                   ALU.add).then_inc(xpb_done, 1)

            def bias_scores(it, j):
                pool.wait_ge(s2_copied, path_count(it, j))
                pool.tensor_tensor(prob[:, j % NPROB, :], prob[:, j % NPROB, :], rel_j[:, kind(j), :],
                                   ALU.add).then_inc(pool_biased, 1)

            pool.wait_ge(d_par, 32)
            pool.wait_ge(zero_ready, 3)
            center(0, 0)
            center(0, 1)
            scale(0, 0)
            add_proj_bias(0, 0)
            scale(0, 1)
            for p in range(2):
                low_part(0, 0, p)
            pool.wait_ge(lo_done, 2 + CREDIT[lo_done])
            fill_rows(1)
            pool.wait_ge(zero_ready, 5)
            for p in range(2):
                low_part(0, 1, p)
            pool.wait_ge(d_xr, 16)
            pool.wait_ge(rel_ready, 8)

            def step(it, j):
                b, w = j // WPI, j % WPI
                if by_pool(j) and live(it, j, NWIN):
                    bias_scores(it, j)
                if w == 3 and live(it, b + 1, B):
                    add_proj_bias(it, b + 1)
                for n in staged(it, j, 8, B + 2):
                    center(it, n)
                for n in staged(it, j, 10, B + 2):
                    scale(it, n)
                for p in range(2):
                    for n in staged(it, j, 16 + p, B):
                        low_part(it, n, p)
                if j == NWIN - 2:
                    center(0, B + 2)
                if j == NWIN:
                    center(0, B + 3)
                if j == NWIN + 1:
                    scale(0, B + 2)

            drive(pool, step)

            def image(it, b):
                if live(it, b + 3, B):
                    center(it, B + b + 3)
                if live(it, b + 2, B):
                    scale(it, B + b + 2)

            drive_images(pool, image)

        @block.vector
        def _(dve):
            def means(it, n):
                if n >= B:
                    after(dve, x2_done, it * 8 + NG * (n - B + 1))
                dve.tensor_reduce(ssum[:, n % 2, :], X[:, norm_cols(it, n)].rearrange("p (w c) -> p w c", c=C),
                                  AX.X, ALU.add).then_inc(sum_done, 1)
                dve.wait_ge(sum_done, it * 2 + n + 1)
                dve.tensor_scalar(mean[:, n % 2, :], ssum[:, n % 2, :], 1.0 / C, None, ALU.mult).then_inc(mean_done, 1)

            def variances(it, n):
                dve.wait_ge(sq_done, it * 2 + n + 1)
                dve.tensor_reduce(vsum[:, n % 2, :], sq[:, n % 2, :].rearrange("p (w c) -> p w c", c=C), AX.X,
                                  ALU.add).then_inc(var_done, 1)
                dve.wait_ge(var_done, it * 2 + n + 1)
                dve.tensor_scalar(var[:, n % 2, :], vsum[:, n % 2, :], 1.0 / C, EPS, ALU.mult,
                                  ALU.add).then_inc(veps_done, 1)

            dve.memset(va[:], 0.0).then_inc(w_ready, 1)
            dve.wait_ge(w_ready, 1)
            dve.memset(va[:].rearrange("p a (n c) -> p (a n) c", c=32)[:, :, HD:HD + 1], 1.0).then_inc(w_ready, 1)
            dve.wait_ge(d_x0, 16)
            means(0, 0)
            dve.wait_ge(d_x1, 16)
            means(0, 1)
            dve.wait_ge(d_par, 32)
            dve.tensor_tensor(wqk_c[:].rearrange("p (a n) -> p a n", a=2), P("wqk").rearrange("p (a n) -> p a n", a=2),
                              P("colscale").unsqueeze(1).to_broadcast([128, 2, 128]), ALU.mult).then_inc(w_ready, 1)
            dve.tensor_copy(b1wide[:], P("b1").to_broadcast([128, 128])).then_inc(w_ready, 1)
            dve.tensor_scalar(wv[:], P("wv"), P("g1"), None, ALU.mult).then_inc(w_ready, 1)
            dve.wait_ge(w_ready, 5)
            dve.tensor_scalar(wqk[:], wqk_c[:], P("g1"), None, ALU.mult).then_inc(w_ready, 1)
            dve.tensor_scalar(w1[:], P("w1"), P("g2"), None, ALU.mult).then_inc(w_ready, 1)
            dve.wait_ge(b_ps, 1)
            dve.scalar_tensor_tensor(qk_bias[:], P("qkb"), P("qks"), pst[0][:, 0:1], ALU.mult,
                                     ALU.add).then_inc(b_ready, 1)
            dve.tensor_tensor(v_bias[:], pst[0][:, 128:256], P("vb"), ALU.add).then_inc(b_ready, 1)
            dve.tensor_tensor(f_bias[:], pst[0][:, 256:257], P("fc1b"), ALU.add).then_inc(b_ready, 1)

            def remainder(it, b, p):
                after(dve, lo_done, it * 4 + 2 * (b - 1) + p + 1)
                dve.wait_ge(hi_done, it * 4 + 2 * b + p + 1)
                dve.scalar_tensor_tensor(rest[:, p, :], pst[1 - p][:], qk_bias[:],
                                         parts[:, b % 2, 0, 512 * p:512 * (p + 1)], ALU.add,
                                         ALU.subtract).then_inc(rest_done, 1)

            def values(it, b):
                dve.wait_ge(vp_done, it * 2 + b + 1 + CREDIT[vp_done])
                after(dve, av_done, it * 32 + 16 * (b - 1))
                dve.tensor_tensor(
                    va[:, b % 2, :].rearrange("p (g n c) -> p g n c", g=NG, c=32)[:, :, :, 0:HD],
                    pst[1][:].rearrange("p (g n c) -> p g n c", g=NG, c=HD),
                    v_bias[:].rearrange("p (n c) -> p n c", c=HD).unsqueeze(1).to_broadcast([128, NG, GW * HEADS, HD]),
                    ALU.add).then_inc(va_done, 1)

            def row_max(it, j):
                if j % GW == 0:
                    after(dve, mT_done, it * 8 + j // GW - 1)
                dve.wait_ge(s1_done, it * 32 + j + 1)
                dve.tensor_reduce(negm[:, (j // GW) % 2, :].rearrange("p (h w) -> p h w", h=HEADS)[:, :, j % GW],
                                  ps1[j % 2][:].rearrange("p (h n) -> p h n", h=HEADS), AX.X, ALU.max,
                                  negate=True).then_inc(max_done, 1)

            def max_parts(it, k):
                after(dve, mT_done, it * 8 + k + 1)
                after(dve, d_mrow[k % 2], it * 128 + 32 * (k // 2))
                t = max_bank(k)[0:HEADS * GW, 0:128]
                dve.tensor_copy(m_hi[:, k % 2, :], t).then_inc(mhi_done, 1)
                dve.wait_ge(mhi_done, it * 8 + k + 1)
                dve.tensor_tensor(m_mid[:, k % 2, :], t, m_hi[:, k % 2, :], ALU.subtract).then_inc(mmid_done, 1)

            variances(0, 0)
            variances(0, 1)
            for p in range(2):
                remainder(0, 0, p)
            for t, dst in enumerate((rel_i, rel_j)):
                dve.wait_ge(rel_ps, t + 1)
                dve.tensor_copy(dst[:, 0, :], ps2[t][:]).then_inc(rel_ready, 1)
                for m in range(3):
                    a = PCOL["mask"][0] + 128 * m
                    dve.tensor_tensor(dst[:, m + 1, :].rearrange("p (h n) -> p h n", h=HEADS),
                                      ps2[t][:].rearrange("p (h n) -> p h n", h=HEADS),
                                      par[:, a:a + 128].unsqueeze(1).to_broadcast([128, HEADS, 128]),
                                      ALU.add).then_inc(rel_ready, 1)
                if t == 0:
                    for p in range(2):
                        remainder(0, 1, p)
            values(0, 0)
            for j in range(LEAD):
                row_max(0, j)
                if j == 4:
                    max_parts(0, 0)
            dve.wait_ge(rel_ready, 8)
            dve.wait_ge(d_xr, 16)

            def step(it, j):
                b, w, k, i = j // WPI, j % WPI, j // GW, j % GW
                for n in staged(it, j, 8, B + 2):
                    means(it, n)
                for n in staged(it, j, 10, B + 2):
                    variances(it, n)
                if live(it, j + LEAD, NWIN):
                    row_max(it, j + LEAD)
                if i == 0 and live(it, k + 1, NGRP):
                    max_parts(it, k + 1)
                if not by_pool(j) and live(it, j, NWIN):
                    dve.wait_ge(s2_done, it * 32 + j + 1 + CREDIT[s2_done])
                    after(dve, av_done, it * 32 + j - NPROB + 1)
                    dve.tensor_tensor(prob[:, j % NPROB, :], ps2[j % 2][:], rel_j[:, kind(j), :],
                                      ALU.add).then_inc(dve_biased, 1)
                if w == 4 and live(it, b + 1, B):
                    values(it, b + 1)
                for p in range(2):
                    for n in staged(it, j, 15 + p, B):
                        remainder(it, n, p)
                if j == NWIN - 2:
                    means(0, B + 2)
                if j == NWIN:
                    variances(0, B + 2)
                    means(0, B + 3)
                if i == 1 and live(it, k - 2, NGRP):
                    after(dve, otok_done, it * 8 + k - 1)
                    o = pch[:, 0:256].rearrange("p (w n) -> p w n", w=GW)
                    dve.reciprocal(rec[:].rearrange("p (w h) -> p w h", w=GW),
                                   o[:, :, HEADS * HD:HEADS * HD + HEADS]).then_inc(rec_done, 1)
                    dve.wait_ge(rec_done, it * 8 + k - 1)
                    dve.tensor_tensor(onorm[:].rearrange("p (w h d) -> p w h d", w=GW, h=HEADS),
                                      o[:, :, 0:HEADS * HD].rearrange("p w (h d) -> p w h d", h=HEADS),
                                      rec[:].rearrange("p (w h) -> p w h", w=GW).unsqueeze(3)
                                      .to_broadcast([128, GW, HEADS, HD]), ALU.mult).then_inc(on_done, 1)
                if i == 3 and live(it, k - 2, NGRP):
                    dve.wait_ge(proj_done, it * 8 + k - 1)
                    dve.wait_ge(xpb_done, it * 2 + (k - 2) // NG + 1)
                    xs = X[:, bass.ds(it * (2 * IMG) + (k - 2) * GW * C, GW * C)]
                    dve.tensor_tensor(xs, xs, pch[:, 0:128], ALU.add).then_inc(x2_done, 1)

            drive(dve, step)

            def mlp_out(it, b):
                after(dve, fc2_done, it * 2 + b + 1)
                after(dve, mlp_done, it * 2 + b)
                dve.tensor_scalar(mT2[:], pav[:], P("fc2b"), None, ALU.add).then_inc(mT2_done, 1)

            def add_residual(it, b):
                dve.wait_ge(mlp_done, it * 2 + b + 1 + CREDIT[mlp_done])
                after(dve, d_out[b % 2], it * 16 + 16 * (b // 2))
                dve.tensor_tensor(res[:, b % 2, :], pch[:], X[:, img_cols(it, b)], ALU.add).then_inc(res_done, 1)

            def image(it, b):
                if live(it, b + 3, B):
                    means(it, B + b + 3)
                mlp_out(it, b - 1)
                if live(it, b + 2, B):
                    variances(it, B + b + 2)
                add_residual(it, b - 1)

            drive_images(dve, image)

        @block.scalar
        def _(act):
            act.wait_ge(credits_ready, 2)

            def copy_yT(it, b):
                act.wait_ge(yTp_done, it * 2 + b + 1 + CREDIT[yTp_done])
                if b < B + 2:
                    after(act, vp_done, it * 2 + b - 1)
                else:
                    act.wait_ge(fc1_done, it * 8 + 4 * (b - B - 1))
                act.activation(yT[:, b % 2, :], pst[0][:], ACT.Copy).then_inc(yT_done, 1)

            def high_part(it, b, p):
                act.wait_ge(qk_done, it * 4 + 2 * b + p + 1)
                after(act, d_scr, it * 192 + 96 * (b - 1))
                act.activation(parts[:, b % 2, 0, 512 * p:512 * (p + 1)], pst[1 - p][:], ACT.Identity,
                               bias=qk_bias[:]).then_inc(hi_done, 1)

            def middle_part(it, b, p):
                act.wait_ge(rest_done, it * 4 + 2 * b + p + 1 + CREDIT[rest_done])
                act.activation(parts[:, b % 2, 1, 512 * p:512 * (p + 1)], rest[:, p, :],
                               ACT.Copy).then_inc(mid_done, 1)

            def square(it, n):
                act.wait_ge(xc_done, it * 2 + n + 1)
                act.activation(sq[:, n % 2, :], xc[:, n % 2, :], ACT.Square).then_inc(sq_done, 1)

            def copy_s2(it, j):
                act.wait_ge(s2_done, it * 32 + j + 1 + CREDIT[s2_done])
                after(act, av_done, it * 32 + j - NPROB + 1)
                act.activation(prob[:, j % NPROB, :], ps2[j % 2][:], ACT.Copy).then_inc(s2_copied, 1)

            def exponential(it, j):
                act.wait_ge(pool_biased if by_pool(j) else dve_biased, path_count(it, j))
                act.activation(prob[:, j % NPROB, :], prob[:, j % NPROB, :], ACT.Exp).then_inc(exp_done, 1)

            def send_max(it, k):
                act.wait_ge(mmid_done, it * 8 + k + 1)
                g = k % NG
                for r, t in enumerate((m_hi, m_mid)):
                    dst = q_rows[KROWS + r:KROWS + r + 1, (k // NG) % 2, :] \
                        .rearrange("p (a g n) -> p a g n", g=NG, n=TOK)[:, :, g, :]
                    act.dma_start(dst, t[:, k % 2, :]).then_inc(d_mrow[k % 2], 16)

            act.wait_ge(d_par, 32)
            act.activation(ident_b[:], P("ident"), ACT.Copy).then_inc(ident_ready, 1)
            square(0, 0)
            square(0, 1)
            act.wait_ge(b_ready, 3)
            for b in range(2):
                copy_yT(0, b)
                for p in range(2):
                    high_part(0, b, p)
                for p in range(2):
                    middle_part(0, b, p)
            send_max(0, 0)

            def gelu(it, b, w):
                act.wait_ge(fc1_done, it * 8 + 4 * b + w + 1)
                after(act, fc2_done, it * 2 + b - 1)
                act.activation(hT[:, 4 * (b % 2) + w, :], (ps1 + ps2)[w][:], ACT.Gelu,
                               bias=f_bias[:]).then_inc(gelu_done, 1)

            def step(it, j):
                b, w, k, i = j // WPI, j % WPI, j // GW, j % GW
                for n in staged(it, j, 9, B + 2):
                    square(it, n)
                if i == 0 and live(it, k - 2, NGRP):
                    act.wait_ge(av_done, it * 32 + GW * (k - 1) + CREDIT[av_done])
                    after(act, otok_done, it * 8 + k - 3)
                    act.activation(oT[:, k % 2, :], pav[:], ACT.Copy).then_inc(oT_done, 1)
                if i == 3 and live(it, k - 2, NGRP):
                    act.wait_ge(onTp_done, it * 8 + k - 1)
                    act.activation(onT[:], pch[:, 0:128], ACT.Copy).then_inc(onT_done, 1)
                if live(it, j - EXP_LAG, NWIN):
                    exponential(it, j - EXP_LAG)
                if by_pool(j) and live(it, j, NWIN):
                    copy_s2(it, j)
                if i == 1 and live(it, k + 1, NGRP):
                    send_max(it, k + 1)
                for n in staged(it, j, 13, B + 1):
                    copy_yT(it, n)
                if j == NWIN:
                    copy_yT(0, B + 1)
                for p in range(2):
                    for n in staged(it, j, 14 + p, B):
                        high_part(it, n, p)
                    for n in staged(it, j, 16 + p, B):
                        middle_part(it, n, p)
                if j in (NWIN - 1, NWIN + 1):
                    square(0, B + 2 + (j > NWIN))
                if j >= NWIN + EXP_LAG and j < NWIN + EXP_LAG + GW:
                    gelu(0, 0, j - NWIN - EXP_LAG)

            drive(act, step)

            def image(it, b):
                if live(it, b, B):
                    gelu(it, b, 0)
                    gelu(it, b, 1)
                if live(it, b + 1, B):
                    copy_yT(it, B + b + 1)
                if live(it, b + 3, B):
                    square(it, B + b + 3)
                if live(it, b, B):
                    gelu(it, b, 2)
                    gelu(it, b, 3)

            drive_images(act, image)

        @block.tensor
        def _(pe):
            pe.wait_ge(credits_ready, 3)
            pe.wait_ge(w_ready, 5)
            pe.matmul(pst[0][:, 0:1], wqk_c[:, 0:128], P("b1"), start=True, stop=True)
            pe.matmul(pst[0][:, 128:256], b1wide[:], P("wv"), start=True, stop=True)
            pe.matmul(pst[0][:, 256:257], P("w1")[:, 0:128], P("b2"), start=True, stop=True).then_inc(b_ps, 1)

            def transpose_y(it, b):
                if b < B:
                    after(pe, rest_done, it * 4 + 2 * b)
                else:
                    after(pe, rest_done, 2 * B)
                    pe.wait_ge(yT_done, it * 2 + b)
                pe.wait_ge(yn_done, it * 2 + b + 1)
                for g in range(NG):
                    mm = pe.transpose(pst[0][:, 128 * g:128 * (g + 1)], yn[:, b % 2, 128 * g:128 * (g + 1)], P("ident"))
                mm.then_inc(yTp_done, 1)

            def project_qk(it, b, p, values):
                if p == 0:
                    after(pe, va_done, values)
                    after(pe, rest_done, it * 4 + 2 * b - 1)
                pe.wait_ge(yT_done, it * 2 + b + 1)
                pe.matmul(pst[1 - p][:], wqk[:, 128 * p:128 * (p + 1)], yT[:, b % 2, :], start=True,
                          stop=True).then_inc(qk_done, 1)

            def project_v(it, b, halves):
                after(pe, rest_done, halves)
                for g in range(NG):
                    mm = pe.matmul(pst[1][:, 128 * g:128 * (g + 1)], yT[:, b % 2, 128 * g:128 * (g + 1)], wv[:],
                                   start=True, stop=True)
                mm.then_inc(vp_done, 1)

            def s1(it, j):
                if (j // GW) % NG == 0 and j % 2 == 0:
                    w = (j % GW) // 2
                    after(pe, d_qk[w], it * 64 + 32 * (j // WPI + 1))
                after(pe, max_done, it * 32 + j - 1)
                c = win_col(j)
                pe.matmul(ps1[j % 2][:], ident_b[:], rel_i[:, kind(j), :], start=True, stop=False)
                for h in range(HEADS):
                    a = HALF * 2 * h + c
                    mm = pe.matmul(ps1[j % 2][:, 128 * h:128 * (h + 1)],
                                   q_rows[0:KROWS, (j // WPI) % 2, a:a + TOK],
                                   k_rows[0:KROWS, (j // WPI) % 2, a:a + TOK], start=False, stop=h == HEADS - 1)
                mm.then_inc(s1_done, 1)

            def s2(it, j):
                if j % GW == 0:
                    after(pe, d_mrow[j // GW % 2], it * 128 + 32 * (j // GW // 2 + 1))
                if j >= 2:
                    pe.wait_ge(s2_copied if by_pool(j - 2) else dve_biased, path_count(it, j - 2))
                c = win_col(j)
                for h in range(HEADS):
                    a = HALF * 2 * h + c
                    mm = pe.matmul(ps2[j % 2][:, 128 * h:128 * (h + 1)],
                                   k_rows[:, (j // WPI) % 2, a:a + TOK],
                                   q_rows[:, (j // WPI) % 2, a:a + TOK], start=True, stop=True)
                mm.then_inc(s2_done, 1)

            def av(it, j):
                k, i = j // GW, j % GW
                if i == 0:
                    after(pe, oT_done, it * 8 + k)
                    if (k % NG) == 0:
                        after(pe, va_done, it * 2 + k // NG + 1)
                after(pe, exp_done, it * 32 + j + 1)
                for h in range(HEADS):
                    a = ((j % WPI) * HEADS + h) * 32
                    mm = pe.matmul(pav[32 * h:32 * (h + 1), 128 * i:128 * (i + 1)],
                                   va[:, (j // WPI) % 2, a:a + 32], prob[:, j % NPROB, 128 * h:128 * (h + 1)],
                                   start=True, stop=True)
                mm.then_inc(av_done, 1)

            def wait_counts(s, count, total):
                pe.wait_ge(s, (min(count, total) if isinstance(count, int) else count) + CREDIT.get(s, 0))

            def transpose_max(it, k):
                b = (k - 1) // NG
                after(pe, mmid_done, it * 8 + k)
                if k % NG == 0:
                    after(pe, va_done, min(b + 2, B) if isinstance(it, int) else it * 2 + b + 2)
                elif k % NG == 1:
                    wait_counts(rest_done, it * 4 + 2 * (b + 1) + 1, 2 * B)
                elif k % NG == 2:
                    wait_counts(rest_done, it * 4 + 2 * (b + 1) + 2, 2 * B)
                    pe.wait_ge(yT_done, it * 2 + b + 2)
                pe.wait_ge(max_done, it * 32 + GW * (k + 1) + CREDIT[max_done])
                pe.transpose(max_bank(k)[0:HEADS * GW, 0:128], negm[:, k % 2, :], P("ident")).then_inc(mT_done, 1)

            pe.wait_ge(w_ready, 6)
            pe.wait_ge(b_ready, 3)
            pe.wait_ge(d_par, 32)
            pe.wait_ge(d_rel, 8 * 16)
            for t in range(2):
                pe.matmul(ps2[t][:], P("flip"), prob[:, t, :], start=True, stop=True).then_inc(rel_ps, 1)
            for b in range(2):
                transpose_y(0, b)
                for p in range(2):
                    project_qk(0, b, p, 0)
            project_v(0, 0, 4)
            pe.wait_ge(rel_ready, 4)
            pe.wait_ge(ident_ready, 1)
            for j in range(LEAD):
                s1(0, j)
                if j == 5:
                    transpose_max(0, 0)

            def fc1(it, b, w):
                if w == 0:
                    pe.wait_ge(yT_done, it * 2 + B + b + 1)
                if isinstance(it, int) and b == 0:
                    if w < 2:
                        after(pe, max_done, NWIN)
                    else:
                        pe.wait_ge(s2_copied if by_pool(NWIN - 4 + w) else dve_biased, path_count(0, NWIN - 4 + w))
                after(pe, gelu_done, it * 8 + 4 * (b - 1) + w + 1)
                pe.matmul((ps1 + ps2)[w][:], w1[:, F * w:F * (w + 1)], yT[:, b % 2, :], start=True,
                          stop=True).then_inc(fc1_done, 1)

            def step(it, j):
                b, w, k, i = j // WPI, j % WPI, j // GW, j % GW
                if live(it, j + LEAD, NWIN):
                    s1(it, j + LEAD)
                if w == 4 and live(it, b + 1, B):
                    pe.wait_ge(mmid_done, it * 8 + k + 1)
                    project_v(it, b + 1, it * 4 + 2 * b + 4)
                if i == 0 and live(it, k + 1, NGRP):
                    transpose_max(it, k + 1)
                if live(it, j, NWIN):
                    s2(it, j)
                if live(it, j - AV_LAG, NWIN):
                    av(it, j - AV_LAG)
                for n in staged(it, j, 13, B + 1):
                    pe.wait_ge(mmid_done, it * 8 + k + 1)
                    transpose_y(it, n)
                if j == NWIN:
                    transpose_y(0, B + 1)
                for p in range(2):
                    for n in staged(it, j, 14 + p, B):
                        pe.wait_ge(mmid_done, it * 8 + k + 2)
                        project_qk(it, n, p, it * 2 + n)
                if i == 1 and live(it, k - 2, NGRP):
                    after(pe, oT_done, it * 8 + k - 1)
                    after(pe, x2_done, it * 8 + k - 2)
                    for u in range(GW):
                        mm = pe.matmul(pch[:, 64 * u:64 * u + HEADS * HD + HEADS],
                                       oT[:, k % 2, 128 * u:128 * (u + 1)], P("sel"), start=True, stop=True)
                    mm.then_inc(otok_done, 1)
                if i == 2 and live(it, k - 2, NGRP):
                    pe.wait_ge(on_done, it * 8 + k - 1)
                    pe.transpose(pch[:, 0:128], onorm[:], P("ident")).then_inc(onTp_done, 1)
                if i == 3 and live(it, k - 2, NGRP):
                    pe.wait_ge(onT_done, it * 8 + k - 1)
                    pe.matmul(pch[:, 0:128], onT[:], P("wp"), start=True, stop=True).then_inc(proj_done, 1)
                if j in (NWIN - 2, NWIN - 1):
                    fc1(0, 0, j - NWIN + 2)
                if j in (NWIN + 1, NWIN + 2):
                    fc1(0, 0, j - NWIN + 1)

            drive(pe, step)

            after(pe, x2_done, NGRP)

            def fc2(it, b):
                after(pe, gelu_done, it * 8 + 4 * (b + 1))
                after(pe, mT2_done, it * 2 + b)
                for w in range(GW):
                    mm = pe.matmul(pav[32 * w:32 * (w + 1), :], P("w2"), hT[:, 4 * (b % 2) + w, :], start=True,
                                   stop=True)
                mm.then_inc(fc2_done, 1)

            def transpose_out(it, b):
                after(pe, mT2_done, it * 2 + b + 1)
                after(pe, res_done, it * 2 + b)
                for g in range(NG):
                    mm = pe.transpose(pch[:, 128 * g:128 * (g + 1)], mT2[:, 128 * g:128 * (g + 1)], P("ident"))
                mm.then_inc(mlp_done, 1)

            def image(it, b):
                if live(it, b, B):
                    fc1(it, b, 0)
                    fc1(it, b, 1)
                fc2(it, b - 1)
                if live(it, b + 1, B):
                    transpose_y(it, B + b + 1)
                if live(it, b, B):
                    fc1(it, b, 2)
                transpose_out(it, b - 1)
                if live(it, b, B):
                    fc1(it, b, 3)

            drive_images(pe, image)


def _to_tokens(x):
    import numpy as np
    x = np.roll(x, (-SHIFT, -SHIFT), axis=(1, 2))
    x = x.reshape(B, NG, WH, GW, WW, C).transpose(2, 4, 0, 1, 3, 5)
    return np.ascontiguousarray(x.reshape(TOK, NWIN * C))


def _from_tokens(y):
    import numpy as np
    y = y.reshape(WH, WW, B, NG, GW, C).transpose(2, 3, 0, 4, 1, 5).reshape(B, H, W, C)
    return np.ascontiguousarray(np.roll(y, (SHIFT, SHIFT), axis=(1, 2)))


def _masks():
    import numpy as np
    y, x = np.divmod(np.arange(TOK), WW)
    below, right = (y >= WH - SHIFT).astype(int), (x >= WW - SHIFT).astype(int)
    return [np.where(r[:, None] != r[None, :], -100.0, 0.0).astype(np.float32)
            for r in (right, below, 2 * below + right)]


def _pack(p):
    import numpy as np
    a = np.zeros((128, NPCOL), np.float32)

    def put(name, v):
        lo, hi = PCOL[name]
        a[:, lo:hi] = v

    for n, k in (("g1", "g1"), ("b1", "b1"), ("g2", "g2"), ("b2", "b2"), ("fc2b", "fc2_b")):
        put(n, np.tile(p[k], GW)[:, None])
    put("fc1b", p["fc1_b"][:, None])
    put("qkb", np.concatenate([np.tile(p["qkv_b"][C * qk:C * (qk + 1)], 2) for qk in range(2)])[:, None])
    scale = np.repeat([SCALE, 1.0], 2 * C).astype(np.float32)
    put("qks", scale[:, None])
    put("colscale", scale[None, :])
    put("vb", np.tile(p["qkv_b"][2 * C:], GW)[None, :])
    put("pb", p["proj_b"][None, :])
    put("ident", np.eye(128, dtype=np.float32))
    put("flip", np.kron(np.eye(WH, dtype=np.float32), np.eye(WW, dtype=np.float32)[::-1]))
    put("mask", np.concatenate(_masks(), 1))
    put("w2", p["fc2_w"])
    wqk, wv, wp = (a[:, PCOL[n][0]:PCOL[n][1]] for n in ("wqk", "wv", "wp"))
    w1, sel = (a[:, PCOL[n][0]:PCOL[n][1]] for n in ("w1", "sel"))
    for w in range(GW):
        rows = slice(C * w, C * (w + 1))
        half, half_w = w % 2, w // 2
        for qk in range(2):
            at = 128 * half + 64 * qk + C * half_w
            wqk[rows, at:at + C] = p["qkv_w"][:, C * qk:C * (qk + 1)]
        wv[rows, C * w:C * (w + 1)] = p["qkv_w"][:, 2 * C:]
        wp[rows, C * w:C * (w + 1)] = p["proj_w"]
        w1[rows, F * w:F * (w + 1)] = p["fc1_w"]
    for h in range(HEADS):
        for d in range(HD):
            sel[32 * h + d, HD * h + d] = 1.0
        sel[32 * h + HD, HEADS * HD + h] = 1.0
    return a


def _runs(rpb):
    import numpy as np
    t = rpb.T.reshape(HEADS, 2 * WH - 1, 2 * WW - 1)
    return [np.ascontiguousarray(np.stack([s[:, WH - 1 - y:2 * WH - 1 - y, :] for y in range(WH)]))
            for s in (t[:, ::-1, ::-1], t)]


def kernel(**inputs):
    import numpy as np
    import concourse.bacc as bacc
    from concourse.bass_utils import run_bass_kernel_spmd

    p = {k.removeprefix("L0_conv_"): np.asarray(v) for k, v in inputs.items()}
    rel_i, rel_j = _runs(p["rpb"])
    arrays = {"x_tok": _to_tokens(p["x"]), "params": _pack(p), "rel_i_runs": rel_i, "rel_j_runs": rel_j}
    nc = bacc.Bacc("TRN2", target_bir_lowering=False, num_devices=1)
    ins = [nc.dram_tensor(k, v.shape, mybir.dt.float32, kind="ExternalInput").ap() for k, v in arrays.items()]
    scratch = nc.dram_tensor("slots", (2, 2, 2, C, NSLOT, HALF), mybir.dt.bfloat16, kind="Internal").ap()
    out = nc.dram_tensor("y_tok", (TOK, NWIN * C), mybir.dt.float32, kind="ExternalOutput").ap()
    swin_kernel(nc, *ins, scratch, out)
    r = run_bass_kernel_spmd(nc, [arrays], core_ids=[0])
    return _from_tokens(r.results[0]["y_tok"])
```

```python
from contextlib import ExitStack

import concourse.bass as bass
from concourse import mybir

B, H, W, C = 8, 16, 128, 32
HEADS, HD = 4, 8
WH, WW, SHIFT = 4, 32, 2
TOK = WH * WW
GW = W // WW
NG = H // WH
WPI = GW * NG
NWIN = B * WPI
NGRP = B * NG
F = 4 * C
HTOK = HEADS * TOK
IMG = WPI * C
SCALE = HD ** -0.5
EPS = 1e-5
NPART = 3
SLOT_PARTS = ((0, 0, 0, 1, 2, 1), (2, 1, 0, 0, 0, 1))
NSLOT = len(SLOT_PARTS[0])
KROWS = HD * NSLOT
MROWS = 2
HALF = WPI // 2 * TOK

_WIDTHS = dict(g1=1, b1=1, g2=1, b2=1, qkb=1, qks=1, fc1b=1, fc2b=1, colscale=128, wqk=256, wv=128,
               ident=128, flip=128, vb=1, wp=128, pb=C, mask=3 * 128, w1=GW * F, w2=C)
PCOL, _at = {}, 0
for _n, _w in _WIDTHS.items():
    PCOL[_n] = (_at, _at + _w)
    _at += _w
NPCOL = _at

ONES_BF16 = 1 + 0x3F80 / 2 ** 23
LEAD = 8
EXP_LAG, AV_LAG = 3, 4
HEAD_STEPS = 8
POOL_WINDOWS = (1, 5, 7, 9, 11, 13, 15)
NPROB = 8
LOOPS = 3
BODY = 2 * WPI
TAIL_STEPS = 8


def swin_kernel(nc, x, params, rel1, rel2, scratch, out):
    fp32, bf16 = mybir.dt.float32, mybir.dt.bfloat16
    ALU, ACT, AX = mybir.AluOpType, mybir.ActivationFunctionType, mybir.AxisListType

    with ExitStack() as ctx:
        def sb(name, shape, dt=fp32):
            return ctx.enter_context(nc.sbuf_tensor(name, shape, dt))

        def sem(name):
            return ctx.enter_context(nc.semaphore(name))

        X = sb("X", [128, NWIN * C])
        par = sb("par", [128, NPCOL])

        def P(name):
            a, b = PCOL[name]
            return par[:, a:b]

        rel_i = sb("rel_i", [128, 4, HTOK], bf16)
        rel_j = sb("rel_j", [128, 4, HTOK])
        ident_b = sb("ident_b", [128, 128], bf16)
        wqk_c = sb("wqk_c", [128, 256])
        wqk = sb("wqk_s", [128, 256])
        wv = sb("wv_s", [128, 128])
        w1 = sb("w1_s", [128, GW * F])
        b1wide = sb("b1wide", [128, 128])
        qk_bias = sb("qk_bias", [128, 1])
        v_bias = sb("v_bias", [128, 128])
        pb = sb("pb_full", [128, C])
        f_bias = sb("f_bias", [128, 1])
        neghalf = sb("neghalf", [128, WPI])
        q_rows = sb("q_rows", [128, 2, HEADS * WPI * TOK], bf16)
        k_rows = sb("k_rows", [128, 2, HEADS * WPI * TOK], bf16)
        parts = sb("parts", [128, 2, NPART, 2 * 512], bf16)
        rest = sb("rest", [128, 2, 512])
        ssum = sb("ssum", [128, 2, WPI])
        mean = sb("mean", [128, 2, WPI])
        vsum = sb("vsum", [128, 2, WPI])
        var = sb("var", [128, 2, WPI])
        rstd = sb("rstd", [128, 2, WPI])
        xc = sb("xc", [128, 2, IMG])
        sq = sb("sq", [128, 2, IMG])
        yn = sb("yn", [128, 2, IMG])
        yT = sb("yT", [128, 2, 512])
        va = sb("va", [128, 2, WPI * HEADS * 32])
        negm = sb("negm", [128, 2, HEADS * GW])
        m_hi = sb("m_hi", [HEADS * GW, 2, 128], bf16)
        m_mid = sb("m_mid", [HEADS * GW, 2, 128], bf16)
        prob = sb("prob", [128, NPROB, HTOK])
        oT = sb("oT", [128, 2, 512])
        rec = sb("rec", [128, GW * HEADS])
        onorm = sb("onorm", [128, 128])
        onT = sb("onT", [128, 128])
        hT = k_rows[:, 0, :].bitcast(fp32).rearrange("p (w n) -> p w n", n=512)
        mT2 = sb("mT2", [128, 512])
        res = sb("res", [128, 2, IMG])

        def bank(name):
            return ctx.enter_context(nc.psum_tensor(name, [128, 512], fp32))

        ps1 = [bank("ps1a"), bank("ps1b")]
        ps2 = [bank("ps2a"), bank("ps2b")]
        pav = bank("pav")
        pch = bank("pch")
        pst = [bank("pst0"), bank("pst1")]

        d_x0, d_x1, d_xr, d_par, d_rel = sem("d_x0"), sem("d_x1"), sem("d_xr"), sem("d_par"), sem("d_rel")
        d_scr, d_out = sem("d_scr"), [sem("d_out0"), sem("d_out1")]
        d_mrow = [sem("d_mrow0"), sem("d_mrow1")]
        d_qk = [sem("d_qk0"), sem("d_qk1")]
        w_ready, b_ps, b_ready, rel_ready, zero_ready = (sem("w_ready"), sem("b_ps"), sem("b_ready"),
                                                         sem("rel_ready"), sem("zero_ready"))
        pb_ps, pb_ready, q0_zero = sem("pb_ps"), sem("pb_ready"), sem("q0_zero")
        credits_ready, rel_ps, ident_ready = sem("credits_ready"), sem("rel_ps"), sem("ident_ready")
        sum_done, mean_done, xc_done, sq_done, var_done = (sem("sum_done"), sem("mean_done"), sem("xc_done"),
                                                           sem("sq_done"), sem("var_done"))
        veps_done, rstd_done, yn_done, xpb_done = sem("veps_done"), sem("rstd_done"), sem("yn_done"), sem("xpb_done")
        yTp_done, yT_done, qk_done, hi_done, rest_done = (sem("yTp_done"), sem("yT_done"), sem("qk_done"),
                                                          sem("hi_done"), sem("rest_done"))
        mid_done, lo_done, vp_done, va_done = sem("mid_done"), sem("lo_done"), sem("vp_done"), sem("va_done")
        s1_done, max_done = sem("s1_done"), sem("max_done")
        mT_done, mhi_done, mmid_done = sem("mT_done"), sem("mhi_done"), sem("mmid_done")
        s2_done, dve_biased = sem("s2_done"), sem("dve_biased")
        s2_copied, pool_biased = sem("s2_copied"), sem("pool_biased")
        exp_done, av_done = sem("exp_done"), sem("av_done")
        oT_done, otok_done, rec_done, on_done = sem("oT_done"), sem("otok_done"), sem("rec_done"), sem("on_done")
        onTp_done, onT_done, proj_done, x2_done = (sem("onTp_done"), sem("onT_done"), sem("proj_done"),
                                                   sem("x2_done"))
        fc1_done, gelu_done = sem("fc1_done"), sem("gelu_done")
        fc2_done, mT2_done, mlp_done, res_done = sem("fc2_done"), sem("mT2_done"), sem("mlp_done"), sem("res_done")

        CREDIT = {max_done: 2, av_done: 4, s2_done: 2 * WPI, mT_done: 2,
                  d_scr: 2 * 96, d_mrow[0]: 32, d_mrow[1]: 32, d_qk[0]: 2 * 32, d_qk[1]: 2 * 32, lo_done: 2,
                  rest_done: 2, va_done: 2, oT_done: 1, otok_done: 2, x2_done: 1, yTp_done: 2, vp_done: 2,
                  gelu_done: 4, fc2_done: 2, mT2_done: 1, res_done: 1, mlp_done: 1,
                  d_out[0]: 16, d_out[1]: 16}

        def after(eng, s, count):
            if isinstance(count, int) and count <= 0:
                return
            eng.wait_ge(s, count + CREDIT.get(s, 0))

        def after_all(eng, *waits):
            values = [c + CREDIT.get(s, 0) for s, c in waits]
            values = [v if isinstance(v, int) else eng.to_reg(v) for v in values]
            for (s, c), v in zip(waits, values):
                if not isinstance(c, int) or c > 0:
                    eng.wait_ge(s, v)

        block = ctx.enter_context(nc.Block())

        def live(it, index, n):
            return not isinstance(it, int) or 0 <= index < n

        def staged(it, j, at, n):
            b = (j - at) // WPI + 2
            return [b] if (j - at) % WPI == 0 and b >= 2 and live(it, b, n) else []

        def drive(eng, step):
            for j in range(HEAD_STEPS):
                step(0, j)
            with eng.Fori(0, LOOPS) as it:
                for j in range(HEAD_STEPS, HEAD_STEPS + BODY):
                    step(it, j)
            for j in range(HEAD_STEPS + LOOPS * BODY, NWIN + TAIL_STEPS):
                step(0, j)

        def drive_images(eng, image):
            with eng.Fori(0, 2) as it:
                image(it, 1)
                image(it, 2)
            for b in range(5, B + 1):
                image(0, b)

        def norm_cols(it, n):
            return bass.ds((it * 2 + n) % B * IMG, IMG)

        def img_cols(it, b):
            return bass.ds(it * (2 * IMG) + b * IMG, IMG)

        def win_col(jw):
            g, wx = (jw // GW) % NG, jw % GW
            return wx * NG * TOK + g * TOK

        def max_bank(k):
            return pst[(1, 1, 0, 1)[k % NG]]

        def by_pool(jw):
            return jw % WPI in POOL_WINDOWS and jw < NWIN - LEAD

        def path_count(it, jw):
            if isinstance(it, int):
                return sum(by_pool(v) == by_pool(jw) for v in range(jw + 1))
            same = [w for w in range(WPI) if (w in POOL_WINDOWS) == by_pool(jw)]
            return it * (2 * len(same)) + jw // WPI * len(same) + sum(w <= jw % WPI for w in same)

        def kind(jw):
            return 2 * ((jw // GW) % NG == NG - 1) + (jw % GW == GW - 1)

        @block.sync
        def _(sp):
            sp.dma_start(X[:, 0:IMG], x[:, 0:IMG]).then_inc(d_x0, 16)
            sp.dma_start(X[:, IMG:2 * IMG], x[:, IMG:2 * IMG]).then_inc(d_x1, 16)
            sp.dma_start(par[:, 0:PCOL["wp"][0]], params[:, 0:PCOL["wp"][0]]).then_inc(d_par, 16)
            sp.dma_start(par[:, PCOL["wp"][0]:], params[:, PCOL["wp"][0]:]).then_inc(d_par, 16)
            for t, src in enumerate((rel1, rel2)):
                for y in range(WH):
                    runs = bass.AP(src.tensor, (y * HEADS * WH) * (2 * WW - 1),
                                   [[1, WW], [2 * WW - 1, HEADS * WH], [1, WW]])
                    sp.dma_start(prob[WW * y:WW * (y + 1), t, :].rearrange("p (a c) -> p a c", c=WW),
                                 runs).then_inc(d_rel, 16)
            sp.dma_start(X[:, 2 * IMG:], x[:, 2 * IMG:]).then_inc(d_xr, 16)
            sp.wait_ge(credits_ready, 1)

            def scatter_parts(it, b):
                after_all(sp, (d_qk[0], it * 64 + 32 * (b - 1)), (d_qk[1], it * 64 + 32 * (b - 1)))
                for part, done in enumerate((hi_done, mid_done, lo_done)):
                    after(sp, done, it * 4 + 2 * (b + 1))
                    for qk in range(2):
                        rows = slice(64 * qk, 64 * qk + 64)
                        slots = [i for i, own in enumerate(SLOT_PARTS[qk]) if own == part]
                        every = slots[1] - slots[0] if len(slots) > 1 else 1
                        src = parts[rows, b % 2, part:part + 1, :].to_broadcast([64, len(slots), 2 * 512])
                        dst = scratch[b % 2, qk, :, :, slots[0]:slots[-1] + 1:every, :] \
                            .rearrange("w r s n -> (w r) s n")
                        sp.dma_start(dst, src).then_inc(d_scr, 16)

            def gather_rows(it, b):
                after_all(sp, (d_scr, it * 192 + 96 * (b + 1)),
                          (s2_done, it * 32 + 16 * (b - 1)))
                for w in range(2):
                    for qk, rows in enumerate((q_rows, k_rows)):
                        dst = rows[0:KROWS, b % 2, :].rearrange("p (h w n) -> p h w n", h=HEADS, w=2)[:, :, w, :]
                        src = scratch[b % 2, qk, w].rearrange("(h d) s n -> (d s) h n", h=HEADS)
                        sp.dma_start(dst, src).then_inc(d_qk[w], 16)

            scatter_parts(0, 0)
            sp.wait_ge(q0_zero, 1)
            gather_rows(0, 0)
            scatter_parts(0, 1)
            sp.wait_ge(zero_ready, 4)
            with sp.Fori(0, LOOPS) as it:
                for b in range(2):
                    gather_rows(it, b + 1)
                    scatter_parts(it, b + 2)
            gather_rows(0, 7)

            def store(it, b):
                after(sp, res_done, it * 2 + b + 1)
                sp.dma_start(out[:, bass.ds(it * (2 * IMG) + b * IMG, IMG)], res[:, b % 2, :]).then_inc(d_out[b], 16)

            with sp.Fori(0, B // 2) as it:
                for b in range(2):
                    store(it, b)
            for b in range(2):
                after(sp, d_out[b], 16 * (B // 2))

        @block.gpsimd
        def _(pool):
            for s, n in CREDIT.items():
                if n:
                    pool.sem_inc(s, n)
            pool.sem_inc(credits_ready, 5)
            pool.memset(neghalf[:], -0.5).then_inc(zero_ready, 1)
            pool.wait_ge(zero_ready, 1)

            def fill_rows(b):
                pool.memset(k_rows[:, b, :].bitcast(fp32), ONES_BF16).then_inc(zero_ready, 1)
                if b:
                    pool.memset(q_rows[:, b, :].bitcast(fp32), 0.0).then_inc(zero_ready, 1)

            fill_rows(0)

            def center(it, n):
                xs = X[:, norm_cols(it, n)].rearrange("p (w c) -> p w c", c=C)
                pool.wait_ge(mean_done, it * 2 + n + 1)
                if n >= 2:
                    pool.wait_ge(yn_done, it * 2 + n - 1)
                pool.tensor_tensor(xc[:, n % 2, :].rearrange("p (w c) -> p w c", c=C), xs,
                                   mean[:, n % 2, :].unsqueeze(2).to_broadcast([128, WPI, C]),
                                   ALU.subtract).then_inc(xc_done, 1)

            def scale(it, n):
                v = lambda t: t[:, n % 2, :].rearrange("p (w c) -> p w c", c=C)
                pool.wait_ge(veps_done, it * 2 + n + 1)
                pool.tensor_tensor(rstd[:, n % 2, :], var[:, n % 2, :], neghalf[:], ALU.pow).then_inc(rstd_done, 1)
                pool.wait_ge(rstd_done, it * 2 + n + 1)
                after(pool, yTp_done, it * 2 + n - 1)
                pool.tensor_tensor(v(yn), v(xc), rstd[:, n % 2, :].unsqueeze(2).to_broadcast([128, WPI, C]),
                                   ALU.mult).then_inc(yn_done, 1)

            def low_part(it, b, p):
                after(pool, mid_done, it * 4 + 2 * b + p + 1)
                pool.tensor_tensor(parts[:, b % 2, 2, 512 * p:512 * (p + 1)], rest[:, p, :],
                                   parts[:, b % 2, 1, 512 * p:512 * (p + 1)], ALU.subtract).then_inc(lo_done, 1)

            def add_proj_bias(it, b):
                xs = X[:, img_cols(it, b)].rearrange("p (w c) -> p w c", c=C)
                pool.tensor_tensor(xs, xs, pb[:].unsqueeze(1).to_broadcast([128, WPI, C]),
                                   ALU.add).then_inc(xpb_done, 1)

            def bias_scores(it, j):
                pool.wait_ge(s2_copied, path_count(it, j))
                pool.tensor_tensor(prob[:, j % NPROB, :], prob[:, j % NPROB, :], rel_j[:, kind(j), :],
                                   ALU.add).then_inc(pool_biased, 1)

            pool.wait_ge(d_par, 32)
            pool.wait_ge(zero_ready, 2)
            center(0, 0)
            center(0, 1)
            scale(0, 0)
            pool.wait_ge(pb_ready, 1)
            add_proj_bias(0, 0)
            scale(0, 1)
            for p in range(2):
                low_part(0, 0, p)
            pool.wait_ge(lo_done, 2 + CREDIT[lo_done])
            fill_rows(1)
            pool.wait_ge(zero_ready, 4)
            for p in range(2):
                low_part(0, 1, p)
            pool.wait_ge(d_xr, 16)
            pool.wait_ge(rel_ready, 8)

            def step(it, j):
                b, w = j // WPI, j % WPI
                if by_pool(j) and live(it, j, NWIN):
                    bias_scores(it, j)
                if w == 6 and live(it, b + 1, B):
                    add_proj_bias(it, b + 1)
                for n in staged(it, j, 0, B + 2):
                    center(it, n)
                for n in staged(it, j, 3, B + 2):
                    scale(it, n)
                for p in range(2):
                    for n in staged(it, j, 13 + p, B):
                        low_part(it, n, p)
                if j == NWIN - 2:
                    center(0, B + 2)
                if j == NWIN:
                    center(0, B + 3)
                if j == NWIN + 1:
                    scale(0, B + 2)

            drive(pool, step)

            def image(it, b):
                if live(it, b + 3, B):
                    center(it, B + b + 3)
                if live(it, b + 2, B):
                    scale(it, B + b + 2)

            drive_images(pool, image)

        @block.vector
        def _(dve):
            def means(it, n, x2_count=None):
                if x2_count is not None:
                    after(dve, x2_done, x2_count)
                after(dve, xc_done, it * 2 + n - 1)
                dve.tensor_reduce(ssum[:, n % 2, :], X[:, norm_cols(it, n)].rearrange("p (w c) -> p w c", c=C),
                                  AX.X, ALU.add).then_inc(sum_done, 1)
                dve.wait_ge(sum_done, it * 2 + n + 1)
                dve.tensor_scalar(mean[:, n % 2, :], ssum[:, n % 2, :], 1.0 / C, None, ALU.mult).then_inc(mean_done, 1)

            def variances(it, n):
                dve.wait_ge(sq_done, it * 2 + n + 1)
                after(dve, rstd_done, it * 2 + n - 1)
                dve.tensor_reduce(vsum[:, n % 2, :], sq[:, n % 2, :].rearrange("p (w c) -> p w c", c=C), AX.X,
                                  ALU.add).then_inc(var_done, 1)
                dve.wait_ge(var_done, it * 2 + n + 1)
                dve.tensor_scalar(var[:, n % 2, :], vsum[:, n % 2, :], 1.0 / C, EPS, ALU.mult,
                                  ALU.add).then_inc(veps_done, 1)

            dve.memset(va[:], 0.0).then_inc(w_ready, 1)
            dve.wait_ge(w_ready, 1)
            dve.memset(va[:].rearrange("p a (n c) -> p (a n) c", c=32)[:, :, HD:HD + 1], 1.0).then_inc(w_ready, 1)
            dve.wait_ge(d_x0, 16)
            means(0, 0)
            dve.wait_ge(d_x1, 16)
            means(0, 1)
            dve.wait_ge(d_par, 32)
            dve.tensor_tensor(wqk_c[:].rearrange("p (a n) -> p a n", a=2), P("wqk").rearrange("p (a n) -> p a n", a=2),
                              P("colscale").unsqueeze(1).to_broadcast([128, 2, 128]), ALU.mult).then_inc(w_ready, 1)
            dve.tensor_copy(b1wide[:], P("b1").to_broadcast([128, 128])).then_inc(w_ready, 1)
            dve.tensor_scalar(wv[:], P("wv"), P("g1"), None, ALU.mult).then_inc(w_ready, 1)
            dve.wait_ge(w_ready, 5)
            dve.tensor_scalar(wqk[:], wqk_c[:], P("g1"), None, ALU.mult).then_inc(w_ready, 1)
            dve.tensor_scalar(w1[:], P("w1"), P("g2"), None, ALU.mult).then_inc(w_ready, 1)
            variances(0, 0)
            dve.wait_ge(b_ps, 1)
            dve.scalar_tensor_tensor(qk_bias[:], P("qkb"), P("qks"), pst[0][:, 0:1], ALU.mult,
                                     ALU.add).then_inc(b_ready, 1)
            dve.tensor_scalar(v_bias[:], pst[0][:, 128:256], P("vb"), None, ALU.add).then_inc(b_ready, 1)
            dve.tensor_tensor(f_bias[:], pst[0][:, 256:257], P("fc1b"), ALU.add).then_inc(b_ready, 1)
            dve.wait_ge(pb_ps, 1)
            dve.tensor_tensor(pb[:], pst[0][:, 0:C], P("pb"), ALU.add).then_inc(pb_ready, 1)

            def remainder(it, b, p):
                after(dve, lo_done, it * 4 + 2 * (b - 1) + p + 1)
                dve.wait_ge(hi_done, it * 4 + 2 * b + p + 1)
                dve.scalar_tensor_tensor(rest[:, p, :], pst[1 - p][:], qk_bias[:],
                                         parts[:, b % 2, 0, 512 * p:512 * (p + 1)], ALU.add,
                                         ALU.subtract).then_inc(rest_done, 1)

            def row_max(it, j):
                if j % GW == 0:
                    after(dve, mT_done, it * 8 + j // GW - 1)
                dve.wait_ge(s1_done, it * 32 + j + 1)
                dve.tensor_reduce(negm[:, (j // GW) % 2, :].rearrange("p (h w) -> p h w", h=HEADS)[:, :, j % GW],
                                  ps1[j % 2][:].rearrange("p (h n) -> p h n", h=HEADS), AX.X, ALU.max,
                                  negate=True).then_inc(max_done, 1)

            def middle_max(it, k):
                dve.wait_ge(mhi_done, it * 8 + k + 1)
                after(dve, d_mrow[k % 2], it * 128 + 32 * (k // 2))
                t = max_bank(k)[0:HEADS * GW, 0:128]
                dve.tensor_tensor(m_mid[:, k % 2, :], t, m_hi[:, k % 2, :], ALU.subtract).then_inc(mmid_done, 1)

            variances(0, 1)
            for p in range(2):
                remainder(0, 0, p)
            for t, dst in enumerate((rel_i, rel_j)):
                dve.wait_ge(rel_ps, t + 1)
                dve.tensor_copy(dst[:, 0, :], ps2[t][:]).then_inc(rel_ready, 1)
                for m in range(3):
                    a = PCOL["mask"][0] + 128 * m
                    dve.tensor_tensor(dst[:, m + 1, :].rearrange("p (h n) -> p h n", h=HEADS),
                                      ps2[t][:].rearrange("p (h n) -> p h n", h=HEADS),
                                      par[:, a:a + 128].unsqueeze(1).to_broadcast([128, HEADS, 128]),
                                      ALU.add).then_inc(rel_ready, 1)
                if t == 0:
                    for p in range(2):
                        remainder(0, 1, p)
            for j in range(LEAD):
                row_max(0, j)
                if j == 4:
                    middle_max(0, 0)
            dve.wait_ge(rel_ready, 8)
            dve.wait_ge(d_xr, 16)

            def step(it, j):
                b, w, k, i = j // WPI, j % WPI, j // GW, j % GW
                for n in staged(it, j, 0, B + 2):
                    means(it, n, it * 8 + k - 2)
                if live(it, j + LEAD, NWIN):
                    row_max(it, j + LEAD)
                if i == 0 and live(it, k + 1, NGRP):
                    middle_max(it, k + 1)
                if not by_pool(j) and live(it, j, NWIN):
                    dve.wait_ge(s2_done, it * 32 + j + 1 + CREDIT[s2_done])
                    after(dve, av_done, it * 32 + j - NPROB + 1)
                    dve.tensor_tensor(prob[:, j % NPROB, :], ps2[j % 2][:], rel_j[:, kind(j), :],
                                      ALU.add).then_inc(dve_biased, 1)
                for n in staged(it, j, 2, B + 2):
                    variances(it, n)
                for p in range(2):
                    for n in staged(it, j, 11 + p, B):
                        remainder(it, n, p)
                if j == NWIN - 2:
                    means(0, B + 2, 3 * NG)
                if j == NWIN:
                    variances(0, B + 2)
                    means(0, B + 3, 4 * NG)
                if i == 1 and live(it, k - 2, NGRP):
                    after(dve, otok_done, it * 8 + k - 1)
                    o = pch[:].rearrange("p (n c) -> p n c", c=32)
                    dve.reciprocal(rec[:].unsqueeze(2), o[:, :, HD:HD + 1]).then_inc(rec_done, 1)
                    dve.wait_ge(rec_done, it * 8 + k - 1)
                    dve.tensor_tensor(onorm[:].rearrange("p (n d) -> p n d", d=HD), o[:, :, 0:HD],
                                      rec[:].unsqueeze(2).to_broadcast([128, GW * HEADS, HD]),
                                      ALU.mult).then_inc(on_done, 1)
                if i == 3 and live(it, k - 2, NGRP):
                    dve.wait_ge(proj_done, it * 8 + k - 1)
                    dve.wait_ge(xpb_done, it * 2 + (k - 2) // NG + 1)
                    xs = X[:, bass.ds(it * (2 * IMG) + (k - 2) * GW * C, GW * C)]
                    dve.tensor_tensor(xs, xs, pch[:, 0:128], ALU.add).then_inc(x2_done, 1)

            drive(dve, step)

            def mlp_out(it, b):
                after(dve, fc2_done, it * 2 + b + 1)
                after(dve, mlp_done, it * 2 + b)
                dve.tensor_scalar(mT2[:], pav[:], P("fc2b"), None, ALU.add).then_inc(mT2_done, 1)

            def add_residual(it, b):
                dve.wait_ge(mlp_done, it * 2 + b + 1 + CREDIT[mlp_done])
                after(dve, d_out[b % 2], it * 16 + 16 * (b // 2))
                dve.tensor_tensor(res[:, b % 2, :], pch[:], X[:, img_cols(it, b)], ALU.add).then_inc(res_done, 1)

            def image(it, b):
                if live(it, b + 3, B):
                    means(it, B + b + 3, it * 8 + NG * (b + 4))
                if live(it, b + 2, B):
                    variances(it, B + b + 2)
                mlp_out(it, b - 1)
                add_residual(it, b - 1)

            drive_images(dve, image)

        @block.scalar
        def _(act):
            act.wait_ge(credits_ready, 2)

            def copy_yT(it, b):
                act.wait_ge(yTp_done, it * 2 + b + 1 + CREDIT[yTp_done])
                if b < B + 2:
                    after(act, vp_done, it * 2 + b - 1)
                else:
                    act.wait_ge(fc1_done, it * 8 + 4 * (b - B - 1))
                act.activation(yT[:, b % 2, :], pst[0][:], ACT.Copy).then_inc(yT_done, 1)

            def high_part(it, b, p):
                act.wait_ge(qk_done, it * 4 + 2 * b + p + 1)
                after(act, d_scr, it * 192 + 96 * (b - 1))
                act.activation(parts[:, b % 2, 0, 512 * p:512 * (p + 1)], pst[1 - p][:], ACT.Identity,
                               bias=qk_bias[:]).then_inc(hi_done, 1)

            def middle_part(it, b, p):
                act.wait_ge(rest_done, it * 4 + 2 * b + p + 1 + CREDIT[rest_done])
                act.activation(parts[:, b % 2, 1, 512 * p:512 * (p + 1)], rest[:, p, :],
                               ACT.Copy).then_inc(mid_done, 1)

            def square(it, n):
                act.wait_ge(xc_done, it * 2 + n + 1)
                after(act, var_done, it * 2 + n - 1)
                act.activation(sq[:, n % 2, :], xc[:, n % 2, :], ACT.Square).then_inc(sq_done, 1)

            def values(it, b):
                act.wait_ge(vp_done, it * 2 + b + 1 + CREDIT[vp_done])
                after(act, av_done, it * 32 + 16 * (b - 1))
                act.activation(va[:, b % 2, :].rearrange("p (n c) -> p n c", c=32)[:, :, 0:HD],
                               pst[1][:].rearrange("p (n c) -> p n c", c=HD), ACT.Copy).then_inc(va_done, 1)

            def copy_s2(it, j):
                act.wait_ge(s2_done, it * 32 + j + 1 + CREDIT[s2_done])
                after(act, av_done, it * 32 + j - NPROB + 1)
                act.activation(prob[:, j % NPROB, :], ps2[j % 2][:], ACT.Copy).then_inc(s2_copied, 1)

            def exponential(it, j):
                act.wait_ge(pool_biased if by_pool(j) else dve_biased, path_count(it, j))
                act.activation(prob[:, j % NPROB, :], prob[:, j % NPROB, :], ACT.Exp).then_inc(exp_done, 1)

            def high_max(it, k):
                after(act, mT_done, it * 8 + k + 1)
                after(act, d_mrow[k % 2], it * 128 + 32 * (k // 2))
                act.activation(m_hi[:, k % 2, :], max_bank(k)[0:HEADS * GW, 0:128], ACT.Copy).then_inc(mhi_done, 1)

            def send_max(it, k):
                act.wait_ge(mmid_done, it * 8 + k + 1)
                g = k % NG
                for r, t in enumerate((m_hi, m_mid)):
                    dst = q_rows[KROWS + r:KROWS + r + 1, (k // NG) % 2, :] \
                        .rearrange("p (a g n) -> p a g n", g=NG, n=TOK)[:, :, g, :]
                    act.dma_start(dst, t[:, k % 2, :]).then_inc(d_mrow[k % 2], 16)

            act.wait_ge(d_par, 32)
            act.activation(ident_b[:], P("ident"), ACT.Copy).then_inc(ident_ready, 1)
            square(0, 0)
            square(0, 1)
            act.wait_ge(zero_ready, 2)
            act.activation(q_rows[:, 0, :].bitcast(fp32), k_rows[:, 0, :].bitcast(fp32), ACT.Copy,
                           scale=0.0).then_inc(q0_zero, 1)
            act.wait_ge(b_ready, 3)
            for b in range(2):
                copy_yT(0, b)
                for p in range(2):
                    high_part(0, b, p)
                for p in range(2):
                    middle_part(0, b, p)
            act.wait_ge(w_ready, 2)
            values(0, 0)
            high_max(0, 0)
            send_max(0, 0)

            def gelu(it, b, w):
                act.wait_ge(fc1_done, it * 8 + 4 * b + w + 1)
                after(act, fc2_done, it * 2 + b - 1)
                act.activation(hT[:, 4 * (b % 2) + w, :], (ps1 + ps2)[w][:], ACT.Gelu,
                               bias=f_bias[:]).then_inc(gelu_done, 1)

            def step(it, j):
                b, w, k, i = j // WPI, j % WPI, j // GW, j % GW
                for n in staged(it, j, 8, B + 2):
                    copy_yT(it, n)
                if i == 0 and live(it, k - 2, NGRP):
                    act.wait_ge(av_done, it * 32 + GW * (k - 1) + CREDIT[av_done])
                    after(act, otok_done, it * 8 + k - 3)
                    act.activation(oT[:, k % 2, :], pav[:], ACT.Copy).then_inc(oT_done, 1)
                if i == 3 and live(it, k - 2, NGRP):
                    act.wait_ge(onTp_done, it * 8 + k - 1)
                    act.activation(onT[:], pch[:, 0:128], ACT.Copy).then_inc(onT_done, 1)
                if i == 0 and live(it, k + 1, NGRP):
                    high_max(it, k + 1)
                if live(it, j - EXP_LAG, NWIN):
                    exponential(it, j - EXP_LAG)
                if by_pool(j) and live(it, j, NWIN):
                    copy_s2(it, j)
                if i == 1 and live(it, k + 1, NGRP):
                    send_max(it, k + 1)
                for n in staged(it, j, 1, B + 2):
                    square(it, n)
                for p in range(2):
                    for n in staged(it, j, 10 + p, B):
                        high_part(it, n, p)
                    for n in staged(it, j, 12 + p, B):
                        middle_part(it, n, p)
                if w == 4 and live(it, b + 1, B):
                    values(it, b + 1)
                if j in (NWIN - 1, NWIN + 1):
                    square(0, B + 2 + (j > NWIN))
                for u in range(2):
                    if NWIN + EXP_LAG <= j < NWIN + EXP_LAG + GW:
                        unit = 2 * (j - NWIN - EXP_LAG) + u
                        gelu(0, unit // GW, unit % GW)

            drive(act, step)

            def image(it, b):
                if live(it, b + 1, B):
                    copy_yT(it, B + b + 1)
                    for w in range(GW):
                        gelu(it, b + 1, w)
                        if w == 1 and live(it, b + 3, B):
                            square(it, B + b + 3)

            drive_images(act, image)

        @block.tensor
        def _(pe):
            pe.wait_ge(credits_ready, 3)
            pe.wait_ge(w_ready, 5)
            pe.matmul(pst[0][:, 0:1], wqk_c[:, 0:128], P("b1"), start=True, stop=True)
            pe.matmul(pst[0][:, 128:256], P("wv"), b1wide[:], start=True, stop=True)
            pe.matmul(pst[0][:, 256:257], P("w1")[:, 0:128], P("b2"), start=True, stop=True).then_inc(b_ps, 1)

            def transpose_y(it, b):
                if b < B:
                    after(pe, rest_done, it * 4 + 2 * b)
                else:
                    after(pe, rest_done, 2 * B)
                    pe.wait_ge(yT_done, it * 2 + b)
                pe.wait_ge(yn_done, it * 2 + b + 1)
                for g in range(NG):
                    mm = pe.transpose(pst[0][:, 128 * g:128 * (g + 1)], yn[:, b % 2, 128 * g:128 * (g + 1)], P("ident"))
                mm.then_inc(yTp_done, 1)

            def project_qk(it, b, p, values):
                if p == 0:
                    after(pe, va_done, values)
                    after(pe, rest_done, it * 4 + 2 * b - 1)
                pe.wait_ge(yT_done, it * 2 + b + 1)
                pe.matmul(pst[1 - p][:], wqk[:, 128 * p:128 * (p + 1)], yT[:, b % 2, :], start=True,
                          stop=True).then_inc(qk_done, 1)

            def project_v(it, b, halves):
                after(pe, rest_done, halves)
                for g in range(NG):
                    mm = pe.matmul(pst[1][:, 128 * g:128 * (g + 1)], yT[:, b % 2, 128 * g:128 * (g + 1)], wv[:],
                                   start=True, stop=True)
                mm.then_inc(vp_done, 1)

            def s1(it, j):
                if (j // GW) % NG == 0 and j % 2 == 0:
                    w = (j % GW) // 2
                    after(pe, d_qk[w], it * 64 + 32 * (j // WPI + 1))
                after(pe, max_done, it * 32 + j - 1)
                c = win_col(j)
                pe.matmul(ps1[j % 2][:], ident_b[:], rel_i[:, kind(j), :], start=True, stop=False)
                for h in range(HEADS):
                    a = HALF * 2 * h + c
                    mm = pe.matmul(ps1[j % 2][:, 128 * h:128 * (h + 1)],
                                   q_rows[0:KROWS, (j // WPI) % 2, a:a + TOK],
                                   k_rows[0:KROWS, (j // WPI) % 2, a:a + TOK], start=False, stop=h == HEADS - 1)
                mm.then_inc(s1_done, 1)

            def s2(it, j):
                if j % GW == 0:
                    after(pe, d_mrow[j // GW % 2], it * 128 + 32 * (j // GW // 2 + 1))
                if j >= 2:
                    pe.wait_ge(s2_copied if by_pool(j - 2) else dve_biased, path_count(it, j - 2))
                c = win_col(j)
                for h in range(HEADS):
                    a = HALF * 2 * h + c
                    mm = pe.matmul(ps2[j % 2][:, 128 * h:128 * (h + 1)],
                                   k_rows[:, (j // WPI) % 2, a:a + TOK],
                                   q_rows[:, (j // WPI) % 2, a:a + TOK], start=True, stop=True)
                mm.then_inc(s2_done, 1)

            def av(it, j):
                k, i = j // GW, j % GW
                if i == 0:
                    after(pe, oT_done, it * 8 + k)
                    if (k % NG) == 0:
                        after(pe, va_done, it * 2 + k // NG + 1)
                after(pe, exp_done, it * 32 + j + 1)
                for h in range(HEADS):
                    a = ((j % WPI) * HEADS + h) * 32
                    mm = pe.matmul(pav[32 * h:32 * (h + 1), 128 * i:128 * (i + 1)],
                                   va[:, (j // WPI) % 2, a:a + 32], prob[:, j % NPROB, 128 * h:128 * (h + 1)],
                                   start=True, stop=True)
                mm.then_inc(av_done, 1)

            def wait_counts(s, count, total):
                pe.wait_ge(s, (min(count, total) if isinstance(count, int) else count) + CREDIT.get(s, 0))

            def transpose_max(it, k):
                b = (k - 1) // NG
                after(pe, mmid_done, it * 8 + k)
                if k % NG == 0:
                    after(pe, va_done, min(b + 2, B) if isinstance(it, int) else it * 2 + b + 2)
                    wait_counts(rest_done, it * 4 + 2 * (b + 2) + (1 if k else 2), 2 * B)
                elif k % NG == 1:
                    wait_counts(rest_done, it * 4 + 2 * (b + 1) + 1, 2 * B)
                elif k % NG == 2:
                    wait_counts(rest_done, it * 4 + 2 * (b + 1) + 2, 2 * B)
                    pe.wait_ge(yT_done, it * 2 + b + 2)
                else:
                    after(pe, va_done, min(b + 2, B) if isinstance(it, int) else it * 2 + b + 2)
                pe.wait_ge(max_done, it * 32 + GW * (k + 1) + CREDIT[max_done])
                pe.transpose(max_bank(k)[0:HEADS * GW, 0:128], negm[:, k % 2, :], P("ident")).then_inc(mT_done, 1)

            pe.wait_ge(w_ready, 6)
            pe.wait_ge(d_par, 32)
            pe.wait_ge(b_ready, 3)
            pe.matmul(pst[0][:, 0:C], v_bias[:], P("wp")[:, 0:C], start=True, stop=True).then_inc(pb_ps, 1)
            pe.wait_ge(d_rel, 8 * 16)
            for t in range(2):
                pe.matmul(ps2[t][:], P("flip"), prob[:, t, :], start=True, stop=True).then_inc(rel_ps, 1)
            pe.wait_ge(pb_ready, 1)
            for b in range(2):
                transpose_y(0, b)
                for p in range(2):
                    project_qk(0, b, p, 0)
            project_v(0, 0, 4)
            pe.wait_ge(rel_ready, 4)
            pe.wait_ge(ident_ready, 1)
            for j in range(LEAD):
                s1(0, j)
                if j == 5:
                    transpose_max(0, 0)

            def fc1(it, b, w):
                if w == 0:
                    pe.wait_ge(yT_done, it * 2 + B + b + 1)
                if isinstance(it, int) and b == 0:
                    if w < 2:
                        after(pe, max_done, NWIN)
                    else:
                        pe.wait_ge(s2_copied if by_pool(NWIN - 4 + w) else dve_biased, path_count(0, NWIN - 4 + w))
                after(pe, gelu_done, it * 8 + 4 * (b - 1) + w + 1)
                pe.matmul((ps1 + ps2)[w][:], w1[:, F * w:F * (w + 1)], yT[:, b % 2, :], start=True,
                          stop=True).then_inc(fc1_done, 1)

            def step(it, j):
                b, w, k, i = j // WPI, j % WPI, j // GW, j % GW
                if live(it, j + LEAD, NWIN):
                    s1(it, j + LEAD)
                if w == 4 and live(it, b + 1, B):
                    pe.wait_ge(mmid_done, it * 8 + k + 1)
                    project_v(it, b + 1, it * 4 + 2 * b + 4)
                if i == 0 and live(it, k + 1, NGRP):
                    transpose_max(it, k + 1)
                if live(it, j, NWIN):
                    s2(it, j)
                if live(it, j - AV_LAG, NWIN):
                    av(it, j - AV_LAG)
                for n in staged(it, j, 7, B + 2):
                    pe.wait_ge(mmid_done, it * 8 + k + 2)
                    transpose_y(it, n)
                for p in range(2):
                    for n in staged(it, j, 9 + p, B):
                        pe.wait_ge(mmid_done, it * 8 + k + 2)
                        project_qk(it, n, p, it * 2 + n)
                if i == 1 and live(it, k - 2, NGRP):
                    after(pe, oT_done, it * 8 + k - 1)
                    after(pe, x2_done, it * 8 + k - 2)
                    for u in range(GW):
                        mm = pe.transpose(pch[:, 128 * u:128 * (u + 1)], oT[:, k % 2, 128 * u:128 * (u + 1)],
                                          P("ident"))
                    mm.then_inc(otok_done, 1)
                if i == 2 and live(it, k - 2, NGRP):
                    pe.wait_ge(on_done, it * 8 + k - 1)
                    pe.transpose(pch[:, 0:128], onorm[:], P("ident")).then_inc(onTp_done, 1)
                if i == 3 and live(it, k - 2, NGRP):
                    pe.wait_ge(onT_done, it * 8 + k - 1)
                    pe.matmul(pch[:, 0:128], onT[:], P("wp"), start=True, stop=True).then_inc(proj_done, 1)
                if j in (NWIN - 2, NWIN - 1):
                    fc1(0, 0, j - NWIN + 2)
                if j in (NWIN, NWIN + 1):
                    fc1(0, 0, j - NWIN + 2)
                if NWIN + 3 <= j < NWIN + 3 + GW:
                    fc1(0, 1, j - NWIN - 3)

            drive(pe, step)

            after(pe, x2_done, NGRP)

            def fc2(it, b):
                after(pe, gelu_done, it * 8 + 4 * (b + 1))
                after(pe, mT2_done, it * 2 + b)
                for w in range(GW):
                    mm = pe.matmul(pav[32 * w:32 * (w + 1), :], P("w2"), hT[:, 4 * (b % 2) + w, :], start=True,
                                   stop=True)
                mm.then_inc(fc2_done, 1)

            def transpose_out(it, b):
                after(pe, mT2_done, it * 2 + b + 1)
                after(pe, res_done, it * 2 + b)
                for g in range(NG):
                    mm = pe.transpose(pch[:, 128 * g:128 * (g + 1)], mT2[:, 128 * g:128 * (g + 1)], P("ident"))
                mm.then_inc(mlp_done, 1)

            def image(it, b):
                ahead = live(it, b + 1, B)
                if ahead:
                    transpose_y(it, B + b + 1)
                fc2(it, b - 1)
                if ahead:
                    fc1(it, b + 1, 0)
                    fc1(it, b + 1, 1)
                transpose_out(it, b - 1)
                if ahead:
                    fc1(it, b + 1, 2)
                    fc1(it, b + 1, 3)

            drive_images(pe, image)


def _to_tokens(x):
    import numpy as np
    x = np.roll(x, (-SHIFT, -SHIFT), axis=(1, 2))
    x = x.reshape(B, NG, WH, GW, WW, C).transpose(2, 4, 0, 1, 3, 5)
    return np.ascontiguousarray(x.reshape(TOK, NWIN * C))


def _from_tokens(y):
    import numpy as np
    y = y.reshape(WH, WW, B, NG, GW, C).transpose(2, 3, 0, 4, 1, 5).reshape(B, H, W, C)
    return np.ascontiguousarray(np.roll(y, (SHIFT, SHIFT), axis=(1, 2)))


def _masks():
    import numpy as np
    y, x = np.divmod(np.arange(TOK), WW)
    below, right = (y >= WH - SHIFT).astype(int), (x >= WW - SHIFT).astype(int)
    return [np.where(r[:, None] != r[None, :], -100.0, 0.0).astype(np.float32)
            for r in (right, below, 2 * below + right)]


def _pack(p):
    import numpy as np
    a = np.zeros((128, NPCOL), np.float32)

    def put(name, v):
        lo, hi = PCOL[name]
        a[:, lo:hi] = v

    for n, k in (("g1", "g1"), ("b1", "b1"), ("g2", "g2"), ("b2", "b2"), ("fc2b", "fc2_b")):
        put(n, np.tile(p[k], GW)[:, None])
    put("fc1b", p["fc1_b"][:, None])
    put("qkb", np.concatenate([np.tile(p["qkv_b"][C * qk:C * (qk + 1)], 2) for qk in range(2)])[:, None])
    scale = np.repeat([SCALE, 1.0], 2 * C).astype(np.float32)
    put("qks", scale[:, None])
    put("colscale", scale[None, :])
    put("vb", np.tile(p["qkv_b"][2 * C:], GW)[:, None])
    put("pb", p["proj_b"][None, :])
    put("ident", np.eye(128, dtype=np.float32))
    put("flip", np.kron(np.eye(WH, dtype=np.float32), np.eye(WW, dtype=np.float32)[::-1]))
    put("mask", np.concatenate(_masks(), 1))
    put("w2", p["fc2_w"])
    wqk, wv, wp = (a[:, PCOL[n][0]:PCOL[n][1]] for n in ("wqk", "wv", "wp"))
    w1 = a[:, PCOL["w1"][0]:PCOL["w1"][1]]
    for w in range(GW):
        rows = slice(C * w, C * (w + 1))
        half, half_w = w % 2, w // 2
        for qk in range(2):
            at = 128 * half + 64 * qk + C * half_w
            wqk[rows, at:at + C] = p["qkv_w"][:, C * qk:C * (qk + 1)]
        wv[rows, C * w:C * (w + 1)] = p["qkv_w"][:, 2 * C:]
        wp[rows, C * w:C * (w + 1)] = p["proj_w"]
        w1[rows, F * w:F * (w + 1)] = p["fc1_w"]
    return a


def _runs(rpb):
    import numpy as np
    t = rpb.T.reshape(HEADS, 2 * WH - 1, 2 * WW - 1)
    return [np.ascontiguousarray(np.stack([s[:, WH - 1 - y:2 * WH - 1 - y, :] for y in range(WH)]))
            for s in (t[:, ::-1, ::-1], t)]


def kernel(**inputs):
    import numpy as np
    import concourse.bacc as bacc
    from concourse.bass_utils import run_bass_kernel_spmd

    p = {k.removeprefix("L0_conv_"): np.asarray(v) for k, v in inputs.items()}
    rel_i, rel_j = _runs(p["rpb"])
    arrays = {"x_tok": _to_tokens(p["x"]), "params": _pack(p), "rel_i_runs": rel_i, "rel_j_runs": rel_j}
    nc = bacc.Bacc("TRN2", target_bir_lowering=False, num_devices=1)
    ins = [nc.dram_tensor(k, v.shape, mybir.dt.float32, kind="ExternalInput").ap() for k, v in arrays.items()]
    scratch = nc.dram_tensor("slots", (2, 2, 2, C, NSLOT, HALF), mybir.dt.bfloat16, kind="Internal").ap()
    out = nc.dram_tensor("y_tok", (TOK, NWIN * C), mybir.dt.float32, kind="ExternalOutput").ap()
    swin_kernel(nc, *ins, scratch, out)
    r = run_bass_kernel_spmd(nc, [arrays], core_ids=[0])
    return _from_tokens(r.results[0]["y_tok"])
```
